# Optimizing a Trainium2 kernel written in Bass

```python
import numpy as np
import jax
import jax.numpy as jnp

def _softmax(x, axis=-1):
    return jax.nn.softmax(x, axis=axis)
def _gelu(x):
    return jax.nn.gelu(x, approximate=True)
def _silu(x):
    return jax.nn.silu(x)
def _sigmoid(x):
    return jax.nn.sigmoid(x)
def _layernorm(x, axis=-1, eps=1e-5):
    m = jnp.mean(x, axis=axis, keepdims=True)
    v = jnp.var(x, axis=axis, keepdims=True)
    return (x - m) / jnp.sqrt(v + eps)
def _scatter_add(tgt, idx, src, axis=0):
    return tgt.at[idx].add(src)
def _segment_sum(src, seg, n):
    return jax.ops.segment_sum(src, seg, n)

kernel_name = 'mk_conv_preact_d1_conv_nchw512_e7bd80'

def setup_inputs(seed: int = 0):
    np.random.seed(seed)
    _w = jnp.asarray
    def _rec_inputs():
        import jax
        import jax.numpy as jnp
        _gk = jax.random.key(seed)
        x = -0.0002928 + 1 * jax.random.normal(jax.random.fold_in(_gk, 1), (8, 512, 32, 32), jnp.float32)
        return x
    x = _rec_inputs()
    def _L0_conv_setup():
        import jax, jax.numpy as jnp
        import numpy as np
        EPS = 1e-05
        NUM_HEADS = 8

        def _expmap0(u):
            n = jnp.linalg.norm(u, axis=-1, keepdims=True)
            scale = jnp.tanh(n) / jnp.maximum(n, 1e-15)
            return u * scale

        def _logmap0(y):
            n = jnp.linalg.norm(y, axis=-1, keepdims=True)
            n_c = jnp.clip(n, 0.0, 1.0 - EPS)
            scale = jnp.arctanh(n_c) / jnp.maximum(n, 1e-15)
            return y * scale

        def _mhsa(x, w_qkv, b_qkv, w_o, b_o):
            B, C, H, W = x.shape
            hd = C // NUM_HEADS
            t = x.reshape(B, C, H * W).transpose(0, 2, 1)
            qkv = t @ w_qkv + b_qkv
            q, k, v = jnp.split(qkv, 3, axis=-1)

            def heads(z):
                return z.reshape(B, H * W, NUM_HEADS, hd).transpose(0, 2, 1, 3)
            q, k, v = (heads(q), heads(k), heads(v))
            scores = jnp.einsum('bhnd,bhmd->bhnm', q, k) / jnp.sqrt(jnp.float32(hd))
            attn = jax.nn.softmax(scores, axis=-1)
            out = jnp.einsum('bhnm,bhmd->bhnd', attn, v)
            out = out.transpose(0, 2, 1, 3).reshape(B, H * W, C)
            out = out @ w_o + b_o
            return out.transpose(0, 2, 1).reshape(B, C, H, W)
        key = jax.random.key(seed)
        ks = jax.random.split(key, 12)
        B, C, H, W = (8, 512, 32, 32)
        hidden = 128
        s_c = 1.0 / np.sqrt(C)
        s_h = 1.0 / np.sqrt(hidden)
        return {'x': jax.random.normal(ks[0], (B, C, H, W), jnp.float32), 'current_step': 1000, 'w1': jax.random.normal(ks[1], (C, hidden), jnp.float32) * s_c, 'b1': jnp.zeros((hidden,), jnp.float32), 'w2': jax.random.normal(ks[2], (hidden, C), jnp.float32) * s_h, 'b2': jnp.zeros((C,), jnp.float32), 'hdn_w_qkv': jax.random.normal(ks[3], (C, 3 * C), jnp.float32) * s_c, 'hdn_b_qkv': jnp.zeros((3 * C,), jnp.float32), 'hdn_w_o': jax.random.normal(ks[4], (C, C), jnp.float32) * s_c, 'hdn_b_o': jnp.zeros((C,), jnp.float32), 'eu_w_qkv': jax.random.normal(ks[5], (C, 3 * C), jnp.float32) * s_c, 'eu_b_qkv': jnp.zeros((3 * C,), jnp.float32), 'eu_w_o': jax.random.normal(ks[6], (C, C), jnp.float32) * s_c, 'eu_b_o': jnp.zeros((C,), jnp.float32)}
    _L0_conv_all = _L0_conv_setup()
    _L0_conv_in = {k: v for k, v in _L0_conv_all.items() if k in ('w1', 'b1', 'w2', 'b2', 'hdn_w_qkv', 'hdn_b_qkv', 'hdn_w_o', 'hdn_b_o', 'eu_w_qkv', 'eu_b_qkv', 'eu_w_o', 'eu_b_o', )}
    del _L0_conv_all

    return {
        "x": x,
        "L0_conv_w1": _L0_conv_in["w1"],
        "L0_conv_b1": _L0_conv_in["b1"],
        "L0_conv_w2": _L0_conv_in["w2"],
        "L0_conv_b2": _L0_conv_in["b2"],
        "L0_conv_hdn_w_qkv": _L0_conv_in["hdn_w_qkv"],
        "L0_conv_hdn_b_qkv": _L0_conv_in["hdn_b_qkv"],
        "L0_conv_hdn_w_o": _L0_conv_in["hdn_w_o"],
        "L0_conv_hdn_b_o": _L0_conv_in["hdn_b_o"],
        "L0_conv_eu_w_qkv": _L0_conv_in["eu_w_qkv"],
        "L0_conv_eu_b_qkv": _L0_conv_in["eu_b_qkv"],
        "L0_conv_eu_w_o": _L0_conv_in["eu_w_o"],
        "L0_conv_eu_b_o": _L0_conv_in["eu_b_o"],
    }

def reference(x, L0_conv_w1, L0_conv_b1, L0_conv_w2, L0_conv_b2, L0_conv_hdn_w_qkv, L0_conv_hdn_b_qkv, L0_conv_hdn_w_o, L0_conv_hdn_b_o, L0_conv_eu_w_qkv, L0_conv_eu_b_qkv, L0_conv_eu_w_o, L0_conv_eu_b_o):
    import jax
    import jax.numpy as jnp
    def _L0_conv_ref(x, current_step, w1, b1, w2, b2, hdn_w_qkv, hdn_b_qkv, hdn_w_o, hdn_b_o, eu_w_qkv, eu_b_qkv, eu_w_o, eu_b_o):
        import jax, jax.numpy as jnp
        import numpy as np
        EPS = 1e-05
        NUM_HEADS = 8

        def _expmap0(u):
            n = jnp.linalg.norm(u, axis=-1, keepdims=True)
            scale = jnp.tanh(n) / jnp.maximum(n, 1e-15)
            return u * scale

        def _logmap0(y):
            n = jnp.linalg.norm(y, axis=-1, keepdims=True)
            n_c = jnp.clip(n, 0.0, 1.0 - EPS)
            scale = jnp.arctanh(n_c) / jnp.maximum(n, 1e-15)
            return y * scale

        def _mhsa(x, w_qkv, b_qkv, w_o, b_o):
            B, C, H, W = x.shape
            hd = C // NUM_HEADS
            t = x.reshape(B, C, H * W).transpose(0, 2, 1)
            qkv = t @ w_qkv + b_qkv
            q, k, v = jnp.split(qkv, 3, axis=-1)

            def heads(z):
                return z.reshape(B, H * W, NUM_HEADS, hd).transpose(0, 2, 1, 3)
            q, k, v = (heads(q), heads(k), heads(v))
            scores = jnp.einsum('bhnd,bhmd->bhnm', q, k) / jnp.sqrt(jnp.float32(hd))
            attn = jax.nn.softmax(scores, axis=-1)
            out = jnp.einsum('bhnm,bhmd->bhnd', attn, v)
            out = out.transpose(0, 2, 1, 3).reshape(B, H * W, C)
            out = out @ w_o + b_o
            return out.transpose(0, 2, 1).reshape(B, C, H, W)
        B, C, H, W = x.shape
        pooled = jnp.mean(x, axis=(2, 3))
        g = jax.nn.relu(pooled @ w1 + b1) @ w2 + b2
        p = jax.nn.sigmoid(g)
        mask = (p > 0.5).astype(x.dtype)
        m = mask[:, :, None, None]
        hyp_feat = x * m
        euc_feat = x * (1.0 - m)
        hyp_out = _logmap0(_mhsa(_expmap0(hyp_feat), hdn_w_qkv, hdn_b_qkv, hdn_w_o, hdn_b_o))
        euc_out = _mhsa(euc_feat, eu_w_qkv, eu_b_qkv, eu_w_o, eu_b_o)
        return hyp_out + euc_out

    def _gn(v, G=32, eps=1e-5):
        B_, C_, H_, W_ = v.shape
        g = v.reshape(B_, G, C_ // G, H_, W_)
        m = jnp.mean(g, axis=(2, 3, 4), keepdims=True)
        s = jnp.var(g, axis=(2, 3, 4), keepdims=True)
        return ((g - m) / jnp.sqrt(s + eps)).reshape(v.shape)

    def _ln_c(v, eps=1e-6):
        m = jnp.mean(v, axis=1, keepdims=True)
        s = jnp.var(v, axis=1, keepdims=True)
        return (v - m) / jnp.sqrt(s + eps)

    def _ln_t(v, eps=1e-5):
        m = jnp.mean(v, axis=-1, keepdims=True)
        s = jnp.var(v, axis=-1, keepdims=True)
        return (v - m) / jnp.sqrt(s + eps)

    def _to_tokens(v):
        B_, C_, H_, W_ = v.shape
        return v.reshape(B_, C_, H_ * W_).transpose(0, 2, 1)
    def _from_tokens(t, like):
        B_, C_, H_, W_ = like.shape
        return t.transpose(0, 2, 1).reshape(B_, C_, H_, W_)

    x = x + _L0_conv_ref(_gn(x), 1000, L0_conv_w1, L0_conv_b1, L0_conv_w2, L0_conv_b2, L0_conv_hdn_w_qkv, L0_conv_hdn_b_qkv, L0_conv_hdn_w_o, L0_conv_hdn_b_o, L0_conv_eu_w_qkv, L0_conv_eu_b_qkv, L0_conv_eu_w_o, L0_conv_eu_b_o)
    return x


_drawn_inputs = setup_inputs


def setup_inputs(seed=0):
    import zlib

    import numpy as np

    out = dict(_drawn_inputs(seed))
    spreads = {'L0_conv_b1': (0.0, 0.1),
     'L0_conv_b2': (0.0, 0.1),
     'L0_conv_hdn_b_qkv': (0.0, 0.1),
     'L0_conv_hdn_b_o': (0.0, 0.1),
     'L0_conv_eu_b_qkv': (0.0, 0.1),
     'L0_conv_eu_b_o': (0.0, 0.1)}
    factors = {}
    for name, (base, spread) in spreads.items():
        noise = np.random.default_rng([zlib.crc32(name.encode()), seed]).standard_normal(out[name].shape)
        drawn = base * np.exp(spread * noise) if base else spread * noise
        out[name] = jnp.asarray(drawn.astype(out[name].dtype))
    for name, factor in factors.items():
        out[name] = (out[name] * factor).astype(out[name].dtype)
    return out
```

```python
import numpy as np
import concourse.bass as bass
from concourse import mybir
from contextlib import ExitStack

F32 = mybir.dt.float32
F32R = mybir.dt.float32r
ALU = mybir.AluOpType
ACT = mybir.ActivationFunctionType
AX = mybir.AxisListType

B, C, H, W = 8, 512, 32, 32
N = H * W
P = 128
HALF = 512
KC = C // P
NT = N // P
HEADS, HD = 8, 64
PAIRS = HEADS // 2
HIDDEN = 128
GROUP = C // 32
SCALE = float(HD) ** -0.5
GN_EPS = 1e-5
EPS = 1e-5
SLOTS_P = 3
TILES = PAIRS * 2 * NT
ROWS = HALF // W

TANH_SERIES = [1.0, -1 / 3, 2 / 15, -17 / 315, 62 / 2835, -1382 / 155925, 21844 / 6081075]
TANH_BELOW = 0.1
ATANH_SERIES = [1.0, 1 / 3, 1 / 5, 1 / 7, 1 / 9, 1 / 11, 1 / 13]
ATANH_BELOW = 0.06

DVE_STEPS = 90
ACT_STEPS = 36


def aux_tiles():
    out = []
    for t in range(2):
        if t == 0:
            out += [((0, "mean"), "D"), ((0, "var"), "D"), ((0, "hidden"), "D"), ((0, "gate"), "D")]
        out += [((t, "v", m), "A") for m in range(NT)]
        out += [((t, "qk", 0, k), "D") for k in range(4)]
        out += [((t, "max", 0, k), "D") for k in range(32)]
        out += [((t, "neg", 0, h), "A") for h in range(2)]
        for g in range(TILES):
            p, r = g // 16, g % 16
            if r == 15 and p + 1 < PAIRS:
                out += [((t, "neg", p + 1, h), "A") for h in range(2)]
            out += [((t,) + f, "D") for f in fillers(g)]
            if g % 8 == 1 and g > 8:
                out += [((t, "den", g // 8 - 1), "D")]
        out += [((t, "den", 2 * PAIRS - 1), "D")]
        out += [((t, "o", k), "AD"[t]) for k in range(8)]
    return out


def fillers(g):
    p, r = g // 16 + 1, g % 16
    if p == PAIRS:
        return []
    if r < 4:
        return [("qk", p, r)]
    return [("max", p, k) for k in range(3 * (r - 4), min(3 * (r - 3), 32))] if r < 15 else []


QK = [(0, 0), (1, 0), (1, 1), (0, 1)]


def build(nc, x, w1, b1, w2, b2, hw_qkv, hb_qkv, hw_o, hb_o, ew_qkv, eb_qkv, ew_o, eb_o, out):
    ctx = ExitStack()
    with ctx:
        ctx.enter_context(nc.allow_non_contiguous_dma(reason="biases, once"))

        def sb(name, shape, dt=F32):
            return ctx.enter_context(nc.sbuf_tensor(name, shape, dt))

        def pb(name, shape):
            return ctx.enter_context(nc.psum_tensor(name, shape, F32))

        def sem(name):
            return ctx.enter_context(nc.semaphore(name))

        x_v = x.rearrange("b (k p) h w -> b k p (h w)", p=P)
        out_v = out.rearrange("b (k p) h w -> b k p (h w)", p=P)
        w_split = nc.dram_tensor("w_split", (16, P, 2048), F32, kind="Internal").ap()

        w_qk = sb("w_qk", [P, 2, KC, 2, P], F32R)
        w_vo = sb("w_vo", [P, 2, 2, 2, C], F32R)
        xs = sb("xs", [P, 2, KC, N], F32R)
        qs = sb("qs", [P, 2, 2, N], F32R)
        qm = sb("qm", [P, 2, 2, N], F32R)
        kk = sb("kk", [P, 2, 2, N], F32R)
        kl = sb("kl", [P, 2, 2, N], F32R)
        v_y = sb("v_y", [P, NT, C])
        probs = sb("probs", [P, SLOTS_P, 2 * HALF])
        psum_v = sb("psum_v", [P, 2 * HALF])
        psum_g = sb("psum_g", [P, 2 * HALF])
        o_t = sb("o_t", [P, 2, PAIRS, N], F32R)
        xin = sb("xin", [P, 2, HALF])
        res = sb("res", [P, 2, HALF])
        tmp = sb("tmp", [P, HALF])
        mxw = sb("mxw", [P, NT, 66], F32R)
        mxp = sb("mxp", [P, 2, NT, 2])
        ident = sb("ident", [P, P], F32R)
        group_mean = sb("group_mean", [P, P])
        ones = sb("ones", [P, HD])
        stats = sb("stats", [P, KC, 2, 6])
        mv = sb("mv", [P, KC, 2])
        gm = sb("gm", [P, KC])
        small = sb("small", [P, 8, KC])
        keep = sb("keep", [P, 2, KC])
        ss = sb("ss", [P, P])
        sc = sb("sc", [P, 4, P])
        bias_q = sb("bias_q", [P, 2, 3, KC])
        bias_o = sb("bias_o", [P, 2, KC])
        bias_1 = sb("bias_1", [P, 1])
        bias_2 = sb("bias_2", [P, KC])

        score_ps = [pb(f"score_ps{i}", [P, 2 * HALF]) for i in range(2)]
        acc_ps = [pb(f"acc_ps{i}", [P, HALF]) for i in range(2)]
        aux_ps = [pb(f"aux_ps{i}", [P, HALF]) for i in range(2)]

        AUX = aux_tiles()
        at = {name: n for n, (name, _) in enumerate(AUX)}
        NAUX = len(AUX)
        assert NAUX % 2 == 0
        upto = {e: [0] for e in "AD"}
        for _, last in AUX:
            for e in "AD":
                upto[e].append(upto[e][-1] + (last == e))
        NFREE = {e: upto[e][-1] for e in "AD"}

        s_const = sem("constants_set")
        s_ident = sem("identity_set")
        s_bias = sem("biases_loaded")
        s_raw = [sem(f"raw_weights_loaded{i}") for i in range(3)]
        s_split = sem("weights_split")
        s_wst = [sem(f"split_weights_stored{i}") for i in range(2)]
        s_wqk = sem("w_qk_loaded")
        s_wvo = sem("w_vo_loaded")
        s_xin = [sem(f"xin_loaded{i}") for i in range(2)]
        s_xfree = sem("xin_read")
        s_xg = sem("x_masked")
        s_xa = sem("x_squared_or_hi")
        s_pe_in = sem("gate_operand_made")
        s_d2a = sem("scale_operand_made")
        s_a2d = sem("scale_function_made")
        s_aux = sem("aux_made")
        s_free = {"A": sem("aux_read_by_scalar"), "D": sem("aux_read_by_vector")}
        s_hi = sem("qk_hi_made")
        s_mx = sem("max_made")
        s_score = sem("scores_made")
        s_exp = sem("probs_made")
        s_pv = sem("probs_multiplied")
        s_sum = [sem("probs_summed_by_vector"), sem("probs_summed_by_gpsimd")]
        s_ln = sem("recip_guessed")
        s_on = sem("o_normal")
        s_ohi = sem("o_hi_made")
        s_olo = sem("o_lo_made")
        s_sq = sem("y_squared")
        s_sqf = sem("y_square_read")
        s_res = [sem(f"residual_loaded{i}") for i in range(2)]
        s_fin = sem("result_made")
        s_out = [sem(f"result_stored{i}") for i in range(2)]
        s_dstep = sem("vector_step")
        s_astep = sem("scalar_step")

        NSC = 2 * TILES
        NSUM = 2 * PAIRS * (NT - 1)
        NX = 32

        def aux_made(eng, i, name):
            eng.wait_ge(s_aux, 1 + i * NAUX + at[name] + 1)
            return aux_ps[at[name] % 2]

        def aux_read(eng, i, name):
            e = AUX[at[name]][1]
            eng.wait_ge(s_free[e], 1 + i * NFREE[e] + upto[e][at[name] + 1])

        def bank_free(pe, i, name):
            n = at[name]
            if n >= 2:
                aux_read(pe, i, AUX[n - 2][0])
            else:
                e = AUX[n - 2][1]
                pe.wait_ge(s_free[e], 1 + i * NFREE[e])
            return aux_ps[n % 2]

        SRCS = []
        for wq, wo in ((hw_qkv, hw_o), (ew_qkv, ew_o)):
            r, ro = (a.rearrange("(k p) n -> p k n", p=P) for a in (wq, wo))
            for p in range(PAIRS):
                SRCS.append([(r[:, :, j * C + p * P:j * C + (p + 1) * P], j) for j in range(2)])
            SRCS += [[(r[:, 2 * c:2 * c + 2, 2 * C:3 * C], None)] for c in range(2)]
            SRCS += [[(ro[:, 2 * c:2 * c + 2, :], None)] for c in range(2)]
        raw_at, count = [], [0] * 3
        for c, parts in enumerate(SRCS):
            count[c % 3] += 16 * len(parts)
            raw_at.append(count[c % 3])

        def token_half(h):
            return slice(h * HALF, (h + 1) * HALF)

        def x_chunk(j):
            return j // 2, token_half(j % 2)

        def sum_tile(eng, i, t, p, h, m):
            g = TILES * t + 16 * p + 8 * h + m
            buf = (psum_v, psum_g)[h]
            n = NSUM // 2 * t + (NT - 1) * p + m - 1
            eng.wait_ge(s_exp, 1 + i * NSC + g + 1)
            if m == 1:
                if p:
                    eng.wait_ge(s_aux, 1 + i * NAUX + at[(t, "den", 2 * (p - 1) + h)] + 1)
                a = probs[:, (g - 1) % SLOTS_P, :]
            else:
                a = buf[:, :]
            eng.wait_ge(s_sum[h], 1 + i * NSUM + n)
            eng.tensor_tensor(buf[:, :], a, probs[:, g % SLOTS_P, :], ALU.add).then_inc(s_sum[h], 1)

        block = ctx.enter_context(nc.Block())

        @block.sync
        def _(sp):
            for q in (s_aux, s_xfree, s_on, s_pv, s_fin, s_mx, s_exp, s_olo, *s_sum, *s_free.values(), *s_out):
                sp.sem_inc(q, 1)
            for t, (bq, bo) in enumerate(((hb_qkv, hb_o), (eb_qkv, eb_o))):
                for j in range(3):
                    sp.dma_start(bias_q[:, t, j, :], bq[j * C:(j + 1) * C].rearrange("(k p) -> p k", p=P)).then_inc(s_bias, 16)
                sp.dma_start(bias_o[:, t, :], bo.rearrange("(k p) -> p k", p=P)).then_inc(s_bias, 16)
            sp.dma_start(bias_1[:, :], b1.rearrange("(p a) -> p a", a=1)).then_inc(s_bias, 16)
            sp.dma_start(bias_2[:, :], b2.rearrange("(k p) -> p k", p=P)).then_inc(s_bias, 16)

            def store_split(c):
                sp.wait_ge(s_split, 2 * c + 2)
                sp.dma_start(w_split[c], o_t[:, c % 2, 0:2, :].rearrange("p a n -> p (a n)").bitcast(F32)).then_inc(s_wst[c % 2], 16)

            for c, parts in enumerate(SRCS):
                if c >= 3:
                    sp.wait_ge(s_split, 2 * (c - 2))
                raw = probs[:, c % 3, :]
                for src, j in parts:
                    dst = (raw.rearrange("p (k n) -> p k n", k=2) if j is None
                           else raw.rearrange("p (k j n) -> p k j n", k=KC, j=2)[:, :, j, :])
                    sp.dma_start(dst, src).then_inc(s_raw[c % 3], 16)
                if c >= 2:
                    store_split(c - 2)
            store_split(14)
            store_split(15)
            for q in s_wst:
                q8 = 16 * 8
                sp.wait_ge(q, q8)
            with sp.Fori(0, B) as i:
                nx = [0]

                def load_x(src, dst3=False):
                    n = nx[0]
                    if n in (10, 11):
                        sp.wait_ge(s_aux, 1 + i * NAUX + at[(0, ("hidden", "gate")[n - 10])] + 1)
                    elif n < 2:
                        sp.wait_ge(s_xfree, 1 + i * NX)
                    else:
                        sp.wait_ge(s_xfree, 1 + i * NX + (n - 1 if n < 10 else n - 3))
                    dst = xin[:, n % 2, :]
                    sp.dma_start(dst.rearrange("p (k n) -> p k n", k=KC) if dst3 else dst,
                                 src).then_inc(s_xin[n % 2], 16)
                    nx[0] += 1

                def load_all_x():
                    for j in range(8):
                        k, cols = x_chunk(j)
                        load_x(x_v[i, k, :, cols])

                def load_vo(c):
                    sp.dma_start(w_vo[:, :, :, :, :].rearrange("p c a k n -> p c (a k n)").bitcast(F32),
                                 w_split[c:c + 2].rearrange("c p n -> p c n")).then_inc(s_wvo, 16)

                def load_qk(c):
                    sp.dma_start(w_qk[:, :, :, :, :].rearrange("p a k j n -> p (a k j n)").bitcast(F32),
                                 w_split[c]).then_inc(s_wqk, 16)

                for t in range(2):
                    if t:
                        sp.wait_ge(s_aux, 1 + i * NAUX + at[(0, "o", 7)] + 1)
                    else:
                        sp.wait_ge(s_aux, 1 + i * NAUX)
                    load_vo(8 * t + 4)
                    load_qk(8 * t)
                    if t == 0:
                        load_all_x()
                        load_x(w1.rearrange("(k p) n -> p k n", p=P), dst3=True)
                        load_x(w2)
                        load_all_x()
                    load_all_x()
                    sp.wait_ge(s_aux, 1 + i * NAUX + at[(t, "v", NT - 1)] + 1)
                    load_vo(8 * t + 6)
                    for p in range(1, PAIRS):
                        sp.wait_ge(s_aux, 1 + i * NAUX + at[(t, "qk", p - 1, 3)] + 1)
                        load_qk(8 * t + p)

                    def tile_of(dram, k):
                        return dram[i, k % 4, :, token_half(k // 4)]

                    def store(k):
                        n = 8 * t + k
                        sp.wait_ge(s_fin, 1 + i * 16 + n + 1)
                        sp.dma_start(tile_of(out_v, k), res[:, n % 2, :]).then_inc(s_out[n % 2], 16)

                    for k in range(8):
                        n = 8 * t + k
                        sp.wait_ge(s_out[n % 2], 1 + i * 128 + 16 * (n // 2))
                        sp.dma_start(res[:, n % 2, :], tile_of((x_v, out_v)[t], k)).then_inc(s_res[n % 2], 16)
                        if k >= 1:
                            store(k - 1)
                    store(7)
            for q in s_out:
                sp.wait_ge(q, 1 + B * 128)

        @block.gpsimd
        def _(pool):
            pool.memset(tmp[:, 0:P], 0.0).then_inc(s_const, 1)
            pool.memset(group_mean[:, :], 1.0 / GROUP).then_inc(s_const, 1)
            pool.memset(ones[:, :], 1.0).then_inc(s_const, 1)
            pool.memset(mxw[:, :, :].bitcast(F32), 0.0).then_inc(s_const, 1)
            pool.memset(qm[:, :, :, :].bitcast(F32), 0.0).then_inc(s_const, 1)
            pool.memset(kl[:, :, :, :].bitcast(F32), 1.0).then_inc(s_const, 1)
            pool.wait_ge(s_const, 6)
            pool.affine_select(out=tmp[:, 0:P], in_=tmp[:, 0:P], compare_op=ALU.not_equal,
                               fill=1.0, base=0, pattern=[[-1, P]], channel_multiplier=1).then_inc(s_const, 1)
            g3 = group_mean[:, :].rearrange("p (g c) -> p g c", c=GROUP)
            pool.affine_select(out=g3, in_=g3, compare_op=ALU.is_ge, fill=0.0, base=0,
                               pattern=[[-GROUP, P // GROUP], [0, GROUP]], channel_multiplier=1).then_inc(s_const, 1)
            pool.wait_ge(s_const, 8)
            pool.affine_select(out=g3, in_=g3, compare_op=ALU.is_ge, fill=0.0, base=GROUP - 1,
                               pattern=[[GROUP, P // GROUP], [0, GROUP]], channel_multiplier=-1).then_inc(s_const, 1)
            with pool.Fori(0, B) as i:
                for t in range(2):
                    for p in range(PAIRS):
                        for m in range(1, NT):
                            sum_tile(pool, i, t, p, 1, m)

        @block.scalar
        def _(act):
            act.wait_ge(s_bias, 16 * 10)
            act.wait_ge(s_ident, 1)
            with act.Fori(0, B) as i:
                steps, d2a = [0], [0]

                def step(ins):
                    steps[0] += 1
                    ins.then_inc(s_astep, 1)
                    act.wait_ge(s_astep, i * ACT_STEPS + steps[0])

                def operand():
                    d2a[0] += 1
                    act.wait_ge(s_d2a, i * 5 + d2a[0])

                def power(dst, src, e):
                    operand()
                    step(act.activation(dst, src, ACT.Ln))
                    act.activation(dst, dst, ACT.Exp, scale=e).then_inc(s_a2d, 1)

                for t in range(2):
                    if t == 0:
                        power(small[:, 3, :], small[:, 2, :], -0.5)
                        for j in range(8):
                            act.wait_ge(s_xg, i * 24 + j + 1)
                            if j:
                                act.wait_ge(s_xfree, 1 + i * NX + 8 + j)
                            else:
                                act.wait_ge(s_on, 1 + i * 16)
                            act.activation(tmp[:, :], xin[:, j % 2, :], ACT.Square).then_inc(s_xa, 1)
                        power(sc[:, 0, :], ss[:, :], -0.5)
                        operand()
                        act.activation(sc[:, 2, :], sc[:, 1, :], ACT.Exp, scale=2.0).then_inc(s_a2d, 1)
                    for j in range(8):
                        k, cols = x_chunk(j)
                        act.wait_ge(s_xg, i * 24 + 8 * (t + 1) + j + 1)
                        act.activation(xs[:, 0, k, cols], xin[:, j % 2, :], ACT.Copy).then_inc(s_xa, 1)

                    def qk_hi(p, k):
                        what, h = QK[k]
                        ps = aux_made(act, i, (t, "qk", p, k))
                        cols = token_half(h)
                        for j, (lo, hi) in enumerate(((0, HD), (HD, P))):
                            b = bias_q[lo:hi, t, what, p:p + 1]
                            dsts = ((qs[lo:hi, p % 2, j, cols], qm[lo:hi, p % 2, j, cols]) if what == 0 else
                                    (kk[0:HD, p % 2, j, cols], kk[HD:P, p % 2, j, cols]))
                            for d in dsts:
                                act.activation(d, ps[lo:hi, :], ACT.Identity, bias=b).then_inc(s_hi, 1)

                    def neg_rows(p):
                        for h in range(2):
                            ps = aux_made(act, i, (t, "neg", p, h))
                            cols = token_half(h)
                            step(act.activation(qm[HD:HD + 1, p % 2, 0, cols], ps[HD:HD + 1, :], ACT.Copy))
                            act.activation(qm[0:1, p % 2, 1, cols], ps[0:1, :], ACT.Copy).then_inc(s_free["A"], 1)

                    def exps(g):
                        n = TILES * t + g
                        act.wait_ge(s_score, i * NSC + n + 1)
                        last = n - SLOTS_P
                        act.wait_ge(s_pv, 1 + i * NSC + max(last + 1, 0))
                        h = (last // 8) % 2
                        need = (NT - 1) * (last // 16) + max(last % 8, 1)
                        act.wait_ge(s_sum[h], 1 + i * NSUM + (need if last >= 0 else 0))
                        act.activation(probs[:, n % SLOTS_P, :], score_ps[n % 2][:, :], ACT.Exp,
                                       scale=SCALE).then_inc(s_exp, 1)

                    def recip_guess(ph):
                        ps = aux_made(act, i, (t, "den", ph))
                        if ph == 0 and t == 0:
                            act.wait_ge(s_xfree, 1 + i * NX + 16)
                        elif ph == 0:
                            act.wait_ge(s_sqf, i * 8 + 8)
                        else:
                            act.wait_ge(s_on, 1 + i * 16 + 8 * t + ph)
                        step(act.activation(tmp[:, :], ps[:, :], ACT.Ln))
                        act.activation(tmp[:, :], tmp[:, :], ACT.Exp, scale=-1.0).then_inc(s_ln, 1)

                    def o_hi(ph):
                        p, h = ph // 2, ph % 2
                        act.wait_ge(s_on, 1 + i * 16 + 8 * t + ph + 1)
                        act.activation(o_t[:, 0, p, token_half(h)], acc_ps[ph % 2][:, :],
                                       ACT.Identity, bias=bias_q[:, t, 2, p:p + 1]).then_inc(s_ohi, 1)

                    for m in range(NT):
                        ps = aux_made(act, i, (t, "v", m))
                        if m == 0:
                            act.wait_ge(s_fin, 1 + i * 16 + 8 * t)
                        act.activation(v_y[:, m, :], ps[:, :], ACT.Copy).then_inc(s_free["A"], 1)
                    for k in range(4):
                        qk_hi(0, k)
                    neg_rows(0)
                    exps(0)
                    for g in range(TILES):
                        p, r = g // 16, g % 16
                        if r == 15 and p + 1 < PAIRS:
                            neg_rows(p + 1)
                        if g + 1 < TILES:
                            exps(g + 1)
                        for f in fillers(g):
                            if f[0] == "qk":
                                qk_hi(f[1], f[2])
                        if g % 8 == 1 and g > 8:
                            recip_guess(g // 8 - 1)
                        if g % 8 == 2 and g > 8:
                            o_hi(g // 8 - 1)
                    recip_guess(2 * PAIRS - 1)
                    o_hi(2 * PAIRS - 1)
                    if t == 0:
                        for k in range(8):
                            ps = aux_made(act, i, (0, "o", k))
                            act.activation(v_y[:, k, :], ps[:, :], ACT.Identity,
                                           bias=bias_o[:, 0, k % 4:k % 4 + 1]).then_inc(s_free["A"], 1)
                            aux_read(act, i, (0, "o", k))
                            if k:
                                act.wait_ge(s_sqf, i * 8 + k)
                            else:
                                act.wait_ge(s_on, 1 + i * 16 + 8)
                            act.activation(tmp[:, :], v_y[:, k, :], ACT.Square).then_inc(s_sq, 1)
                        power(sc[:, 0, :], ss[:, :], -0.5)
                        operand()
                        step(act.activation(sc[:, 2, :], sc[:, 1, :], ACT.Ln, bias=1.0))
                        act.activation(sc[:, 3, :], sc[:, 1, :], ACT.Ln, bias=1.0, scale=-1.0).then_inc(s_a2d, 1)
                assert (steps[0], d2a[0]) == (ACT_STEPS, 5), ("ACT_STEPS", steps[0], d2a[0])

        @block.vector
        def _(dve):
            for c in range(len(SRCS)):
                dve.wait_ge(s_raw[c % 3], raw_at[c])
                if c >= 2:
                    dve.wait_ge(s_wst[c % 2], 16 * (c // 2))
                dve.tensor_copy(o_t[:, c % 2, 0, :], probs[:, c % 3, :]).then_inc(s_split, 1)
                dve.wait_ge(s_split, 2 * c + 1)
                dve.tensor_tensor(o_t[:, c % 2, 1, :], probs[:, c % 3, :], o_t[:, c % 2, 0, :].bitcast(F32),
                                  ALU.subtract).then_inc(s_split, 1)
            dve.wait_ge(s_const, 9)
            dve.tensor_copy(ident[:, :], tmp[:, 0:P]).then_inc(s_ident, 1)
            dve.wait_ge(s_ident, 1)
            dve.wait_ge(s_bias, 16 * 10)
            with dve.Fori(0, B) as i:
                steps, a2d, nx, pe_in = [0], [0], [0], [0]

                def step(ins):
                    steps[0] += 1
                    ins.then_inc(s_dstep, 1)
                    dve.wait_ge(s_dstep, i * DVE_STEPS + steps[0])

                def function():
                    a2d[0] += 1
                    dve.wait_ge(s_a2d, i * 5 + a2d[0])

                def chunk_in():
                    n = nx[0]
                    nx[0] += 1
                    dve.wait_ge(s_xin[n % 2], i * 16 * 17 + 16 * (n // 2 + 1))
                    return xin[:, n % 2, :]

                def newton_rsqrt(r, v, work):
                    step(dve.tensor_tensor(work, r, r, ALU.mult))
                    step(dve.tensor_tensor(work, work, v, ALU.mult))
                    step(dve.scalar_tensor_tensor(work, work, 3.0, r, ALU.subtract, ALU.mult))
                    step(dve.tensor_scalar(r, work, -0.5, None, ALU.mult))

                def series(dst, s, coefs):
                    step(dve.tensor_scalar(dst, s, coefs[-1], None, ALU.mult))
                    for c in coefs[-2:0:-1]:
                        step(dve.scalar_tensor_tensor(dst, dst, c, s, ALU.add, ALU.mult))
                    step(dve.tensor_scalar(dst, dst, coefs[0], None, ALU.add))

                def blend(dst, small_one, s, below):
                    step(dve.tensor_scalar(s, s, below, None, ALU.is_lt))
                    step(dve.tensor_tensor(small_one, small_one, dst, ALU.subtract))
                    step(dve.tensor_tensor(small_one, small_one, s, ALU.mult))
                    step(dve.tensor_tensor(dst, dst, small_one, ALU.add))

                def rows(ap):
                    return ap.rearrange("p (r w) -> p r w", w=W)

                def per_row(a, k0):
                    return sc[:, a, k0:k0 + ROWS].unsqueeze(2).to_broadcast([P, ROWS, W])

                for t in range(2):
                    if t == 0:
                        for j in range(8):
                            chunk = chunk_in()
                            dve.bn_stats(stats[:, j // 2, j % 2, :], chunk).then_inc(s_xfree, 1)
                        dve.wait_ge(s_xfree, 1 + i * NX + 8)
                        dve.memset(small[:, 7, :], 0.0)
                        for k in range(KC - 1):
                            dve.bn_aggr(mv[:, k, :], stats[:, k, :, :].rearrange("p h s -> p (h s)"))
                        dve.bn_aggr(mv[:, KC - 1, :], stats[:, KC - 1, :, :].rearrange("p h s -> p (h s)")).then_inc(s_pe_in, 1)
                        ps = aux_made(dve, i, (0, "mean"))
                        dve.tensor_copy(gm[:, :], ps[:, 0:KC]).then_inc(s_free["D"], 1)
                        aux_read(dve, i, (0, "mean"))
                        step(dve.tensor_tensor(small[:, 1, :], mv[:, :, 0], gm[:, :], ALU.subtract))
                        step(dve.tensor_tensor(small[:, 0, :], small[:, 1, :], small[:, 1, :], ALU.mult))
                        dve.tensor_tensor(small[:, 0, :], small[:, 0, :], mv[:, :, 1], ALU.add).then_inc(s_pe_in, 1)
                        ps = aux_made(dve, i, (0, "var"))
                        step(dve.tensor_scalar(small[:, 2, :], ps[:, 0:KC], GN_EPS, None, ALU.add))
                        dve.tensor_copy(small[:, 5, :], ps[:, 0:KC]).then_inc(s_free["D"], 1)
                        dve.tensor_copy(small[:, 6, :], small[:, 2, :]).then_inc(s_d2a, 1)
                        function()
                        newton_rsqrt(small[:, 3, :], small[:, 2, :], small[:, 4, :])
                        dve.tensor_tensor(small[:, 0, :], small[:, 1, :], small[:, 3, :], ALU.mult).then_inc(s_pe_in, 1)
                        ps = aux_made(dve, i, (0, "hidden"))
                        nx[0] += 1
                        dve.tensor_scalar(small[:, 4, 0:1], ps[:, 0:1], bias_1[:, 0:1], None, ALU.add).then_inc(s_free["D"], 1)
                        aux_read(dve, i, (0, "hidden"))
                        dve.tensor_scalar(small[:, 5, 0:1], small[:, 4, 0:1], 0.0, None, ALU.max).then_inc(s_pe_in, 1)
                        ps = aux_made(dve, i, (0, "gate"))
                        nx[0] += 1
                        dve.tensor_tensor(small[:, 4, :], ps[:, 0:KC], bias_2[:, :], ALU.add).then_inc(s_free["D"], 1)
                        aux_read(dve, i, (0, "gate"))
                        step(dve.tensor_scalar(small[:, 5, :], small[:, 4, :], 0.0, None, ALU.is_gt))
                        step(dve.tensor_tensor(keep[:, 0, :], small[:, 3, :], small[:, 5, :], ALU.mult))
                        step(dve.tensor_tensor(keep[:, 1, :], small[:, 3, :], keep[:, 0, :], ALU.subtract))
                        for j in range(8):
                            k = j // 2
                            chunk = chunk_in()
                            dve.tensor_scalar(chunk, chunk, gm[:, k:k + 1], keep[:, 0, k:k + 1],
                                              ALU.subtract, ALU.mult).then_inc(s_xg, 1)
                            dve.wait_ge(s_xa, i * 24 + j + 1)
                            dve.tensor_reduce(ss[:, j * ROWS:(j + 1) * ROWS], rows(tmp[:, :]), AX.X,
                                              ALU.add).then_inc(s_xfree, 1)
                        dve.wait_ge(s_xfree, 1 + i * NX + 16)
                        dve.tensor_scalar(ss[:, :], ss[:, :], 2.0 ** -60, None, ALU.max).then_inc(s_d2a, 1)
                        function()
                        newton_rsqrt(sc[:, 0, :], ss[:, :], sc[:, 1, :])
                        step(dve.tensor_tensor(sc[:, 1, :], ss[:, :], sc[:, 0, :], ALU.mult))
                        dve.tensor_scalar(sc[:, 1, :], sc[:, 1, :], 20.0, None, ALU.min).then_inc(s_d2a, 1)
                        function()
                        step(dve.tensor_scalar(sc[:, 2, :], sc[:, 2, :], 1.0, None, ALU.add))
                        step(dve.reciprocal(sc[:, 3, :], sc[:, 2, :]))
                        step(dve.tensor_scalar(sc[:, 3, :], sc[:, 3, :], -2.0, 1.0, ALU.mult, ALU.add))
                        step(dve.tensor_tensor(sc[:, 3, :], sc[:, 3, :], sc[:, 0, :], ALU.mult))
                        step(dve.tensor_scalar(ss[:, :], ss[:, :], 1.0, None, ALU.min))
                        series(sc[:, 1, :], ss[:, :], TANH_SERIES)
                        blend(sc[:, 3, :], sc[:, 1, :], ss[:, :], TANH_BELOW)
                    for j in range(8):
                        k, cols = x_chunk(j)
                        chunk = chunk_in()
                        norm = dve.tensor_scalar(chunk, chunk, gm[:, k:k + 1], keep[:, t, k:k + 1], ALU.subtract, ALU.mult)
                        if t == 0:
                            step(norm)
                            dve.tensor_tensor(rows(chunk), rows(chunk), per_row(3, j * ROWS), ALU.mult).then_inc(s_xg, 1)
                        else:
                            norm.then_inc(s_xg, 1)
                        dve.wait_ge(s_xa, i * 24 + 8 * (t + 1) + j + 1)
                        dve.tensor_tensor(xs[:, 1, k, cols], chunk, xs[:, 0, k, cols].bitcast(F32),
                                          ALU.subtract).then_inc(s_xfree, 1)

                    def qk_lo(p, k):
                        what, h = QK[k]
                        ps = aux_made(dve, i, (t, "qk", p, k))
                        n = 16 * t + 4 * p + k
                        dve.wait_ge(s_hi, i * 128 + 4 * (n + 1))
                        cols = token_half(h)
                        for j, (lo, hi) in enumerate(((0, HD), (HD, P))):
                            high = (qs, kk)[what][lo:hi, p % 2, j, cols].bitcast(F32)
                            dst = qs[P - hi:P - lo, p % 2, j, cols] if what == 0 else kl[lo:hi, p % 2, j, cols]
                            ins = dve.scalar_tensor_tensor(dst, ps[lo:hi, :], bias_q[lo:hi, t, what, p:p + 1], high,
                                                           ALU.add, ALU.subtract)
                        ins.then_inc(s_free["D"], 1)

                    def max_tile(p, k):
                        j, n, h = k // 16, (k // 2) % 8, k % 2
                        ps = aux_made(dve, i, (t, "max", p, k))
                        if k == 0:
                            dve.wait_ge(s_mx, 1 + i * 16 + 8 * t + 2 * p)
                        dve.tensor_reduce(mxp[:, j, n, h:h + 1], ps[:, :], AX.X, ALU.max).then_inc(s_free["D"], 1)

                    def combine(p):
                        aux_read(dve, i, (t, "max", p, 31))
                        for j in range(2):
                            dve.tensor_reduce(mxw[:, :, HD * (1 - j)], mxp[:, j, :, :], AX.X, ALU.max,
                                              negate=True).then_inc(s_mx, 1)

                    def normalise(ph):
                        ps = aux_made(dve, i, (t, "den", ph))
                        n = 8 * t + ph
                        dve.wait_ge(s_ln, i * 16 + n + 1)
                        step(dve.tensor_tensor(ps[:, :], ps[:, :], tmp[:, :], ALU.mult))
                        dve.scalar_tensor_tensor(tmp[:, :], ps[:, :], 2.0, tmp[:, :], ALU.subtract,
                                                 ALU.mult).then_inc(s_free["D"], 1)
                        aux_read(dve, i, (t, "den", ph))
                        acc = acc_ps[ph % 2]
                        dve.scalar_tensor_tensor(acc[:, :], acc[:, :], -1.0, tmp[:, :], ALU.mult,
                                                 ALU.mult).then_inc(s_on, 1)

                    def o_lo(ph):
                        p, h = ph // 2, ph % 2
                        dve.wait_ge(s_ohi, i * 16 + 8 * t + ph + 1)
                        dve.scalar_tensor_tensor(o_t[:, 1, p, token_half(h)], acc_ps[ph % 2][:, :],
                                                 bias_q[:, t, 2, p:p + 1], o_t[:, 0, p, token_half(h)].bitcast(F32),
                                                 ALU.add, ALU.subtract).then_inc(s_olo, 1)

                    for k in range(4):
                        qk_lo(0, k)
                    for k in range(32):
                        max_tile(0, k)
                    combine(0)
                    for g in range(TILES):
                        p, r = g // 16, g % 16
                        for f in fillers(g):
                            if f[0] == "qk":
                                qk_lo(f[1], f[2])
                            else:
                                max_tile(f[1], f[2])
                        if r == 14 and p + 1 < PAIRS:
                            combine(p + 1)
                        if r < 8 and r:
                            sum_tile(dve, i, t, p, 0, r)
                        if g % 8 == 1 and g > 8:
                            normalise(g // 8 - 1)
                        if g % 8 == 3 and g > 8:
                            o_lo(g // 8 - 1)
                    normalise(2 * PAIRS - 1)
                    o_lo(2 * PAIRS - 1)
                    if t == 0:
                        for k in range(8):
                            dve.wait_ge(s_sq, i * 8 + k + 1)
                            dve.tensor_reduce(ss[:, k * ROWS:(k + 1) * ROWS], rows(tmp[:, :]), AX.X,
                                              ALU.add).then_inc(s_sqf, 1)
                        dve.wait_ge(s_sqf, i * 8 + 8)
                        dve.tensor_scalar(ss[:, :], ss[:, :], 2.0 ** -60, None, ALU.max).then_inc(s_d2a, 1)
                        function()
                        newton_rsqrt(sc[:, 0, :], ss[:, :], sc[:, 1, :])
                        step(dve.tensor_tensor(sc[:, 1, :], ss[:, :], sc[:, 0, :], ALU.mult))
                        dve.tensor_scalar(sc[:, 1, :], sc[:, 1, :], float(np.float32(1.0) - np.float32(EPS)), None,
                                          ALU.min).then_inc(s_d2a, 1)
                        function()
                        step(dve.tensor_tensor(sc[:, 3, :], sc[:, 2, :], sc[:, 3, :], ALU.subtract))
                        step(dve.scalar_tensor_tensor(sc[:, 3, :], sc[:, 3, :], 0.5, sc[:, 0, :], ALU.mult, ALU.mult))
                        step(dve.tensor_scalar(ss[:, :], ss[:, :], 1.0, None, ALU.min))
                        series(sc[:, 1, :], ss[:, :], ATANH_SERIES)
                        blend(sc[:, 3, :], sc[:, 1, :], ss[:, :], ATANH_BELOW)
                        for k in range(8):
                            y = v_y[:, k, :]
                            step(dve.tensor_tensor(rows(y), rows(y), per_row(3, k * ROWS), ALU.mult))
                            dve.wait_ge(s_res[k % 2], i * 128 + 16 * (k // 2 + 1))
                            dve.tensor_tensor(res[:, k % 2, :], res[:, k % 2, :], y, ALU.add).then_inc(s_fin, 1)
                    else:
                        for k in range(8):
                            ps = aux_made(dve, i, (1, "o", k))
                            dve.wait_ge(s_res[k % 2], i * 128 + 64 + 16 * (k // 2 + 1))
                            r = res[:, k % 2, :]
                            step(dve.scalar_tensor_tensor(r, ps[:, :], bias_o[:, 1, k % 4:k % 4 + 1], r,
                                                          ALU.add, ALU.add))
                            dve.tensor_copy(small[:, 6, 0:1], small[:, 6, 0:1]).then_inc(s_free["D"], 1)
                            dve.tensor_copy(small[:, 7, 0:1], small[:, 7, 0:1]).then_inc(s_fin, 1)
                assert (steps[0], a2d[0], nx[0]) == (DVE_STEPS, 5, 34), ("DVE_STEPS", steps[0], a2d[0], nx[0])

        @block.tensor
        def _(pe):
            pe.wait_ge(s_const, 9)
            pe.wait_ge(s_ident, 1)
            with pe.Fori(0, B) as i:

                def halves(ps, lhs, rhs):
                    todo = [(k, a, b) for k in range(KC) for a, b in ((0, 0), (0, 1), (1, 0))]
                    for n, (k, a, b) in enumerate(todo):
                        last = nc.tensor.matmul(ps, lhs(a, k), rhs(b, k), start=(n == 0), stop=(n == len(todo) - 1))
                    return last

                def gate():
                    ps = bank_free(pe, i, (0, "mean"))
                    pe.wait_ge(s_pe_in, i * 4 + 1)
                    nc.tensor.matmul(ps[:, 0:KC], group_mean[:, :], mv[:, :, 0], start=True, stop=True).then_inc(s_aux, 1)
                    ps = bank_free(pe, i, (0, "var"))
                    pe.wait_ge(s_pe_in, i * 4 + 2)
                    nc.tensor.matmul(ps[:, 0:KC], group_mean[:, :], small[:, 0, :], start=True, stop=True).then_inc(s_aux, 1)
                    ps = bank_free(pe, i, (0, "hidden"))
                    pe.wait_ge(s_pe_in, i * 4 + 3)
                    pe.wait_ge(s_xin[0], i * 16 * 17 + 16 * 5)
                    for k in range(KC):
                        last = nc.tensor.matmul(ps[:, 0:1], xin[:, 0, k * HIDDEN:(k + 1) * HIDDEN], small[:, 0, k:k + 1],
                                                start=(k == 0), stop=(k == KC - 1))
                    last.then_inc(s_aux, 1)
                    ps = bank_free(pe, i, (0, "gate"))
                    pe.wait_ge(s_pe_in, i * 4 + 4)
                    pe.wait_ge(s_xin[1], i * 16 * 17 + 16 * 5)
                    for k in range(KC):
                        last = nc.tensor.matmul(ps[:, k:k + 1], xin[:, 1, k * P:(k + 1) * P], small[:, 5, 0:1],
                                                start=True, stop=True)
                    last.then_inc(s_aux, 1)

                for t in range(2):
                    if t == 0:
                        gate()
                    pe.wait_ge(s_wvo, i * 64 + 32 * t + 16)
                    pe.wait_ge(s_xfree, 1 + i * NX + 16 + 8 * (t + 1))
                    for m in range(NT):
                        ps = bank_free(pe, i, (t, "v", m))
                        halves(ps[:, :], lambda a, k: xs[:, a, k, m * P:(m + 1) * P],
                               lambda b, k: w_vo[:, k // 2, b, k % 2, :]).then_inc(s_aux, 1)

                    def qk_tile(p, k):
                        what, h = QK[k]
                        ps = bank_free(pe, i, (t, "qk", p, k))
                        if k == 0:
                            pe.wait_ge(s_wqk, i * 128 + 16 * (4 * t + p + 1))
                        halves(ps[:, :], lambda a, c: w_qk[:, a, c, what, :],
                               lambda b, c: xs[:, b, c, token_half(h)]).then_inc(s_aux, 1)

                    def max_tile(p, k):
                        j, n, h = k // 16, (k // 2) % 8, k % 2
                        ps = bank_free(pe, i, (t, "max", p, k))
                        if k == 0:
                            aux_read(pe, i, (t, "qk", p, 3))
                        nc.tensor.matmul(ps[:, :], qs[:, p % 2, j, n * P:(n + 1) * P], kk[:, p % 2, j, token_half(h)],
                                         start=True, stop=True).then_inc(s_aux, 1)

                    def neg_rows(p):
                        pe.wait_ge(s_mx, 1 + i * 16 + 8 * t + 2 * (p + 1))
                        for h in range(2):
                            ps = bank_free(pe, i, (t, "neg", p, h))
                            for n in range(4):
                                last = nc.tensor.matmul(ps[0:HD + 1, n * P:(n + 1) * P], mxw[:, 4 * h + n, 0:HD + 1],
                                                        ident[:, :], start=True, stop=True)
                            last.then_inc(s_aux, 1)

                    def scores(g):
                        p, h, m = g // 16, (g // 8) % 2, g % 8
                        n = TILES * t + g
                        if g % 16 == 0:
                            aux_read(pe, i, (t, "neg", p, 1))
                        pe.wait_ge(s_exp, 1 + i * NSC + max(n - 1, 0))
                        ps = score_ps[n % 2]
                        for j in range(2):
                            o = ps[:, token_half(j)]
                            nc.tensor.matmul(o, kk[:, p % 2, j, m * P:(m + 1) * P], qs[:, p % 2, j, token_half(h)],
                                             start=True, stop=False)
                            last = nc.tensor.matmul(o, kl[:, p % 2, j, m * P:(m + 1) * P], qm[:, p % 2, j, token_half(h)],
                                                    start=False, stop=True)
                        last.then_inc(s_score, 1)

                    def prob_v(g):
                        p, ph, m = g // 16, g // 8, g % 8
                        n = TILES * t + g
                        pe.wait_ge(s_exp, 1 + i * NSC + n + 1)
                        if m == 0:
                            pe.wait_ge(s_olo, 1 + i * 16 + max(8 * t + ph - 1, 0))
                        for j in range(2):
                            head = slice((2 * p + j) * HD, (2 * p + j + 1) * HD)
                            last = nc.tensor.matmul(acc_ps[ph % 2][j * HD:(j + 1) * HD, :], v_y[:, m, head],
                                                    probs[:, n % SLOTS_P, token_half(j)],
                                                    start=(m == 0), stop=(m == NT - 1))
                        last.then_inc(s_pv, 1)

                    def denominator(ph):
                        h = ph % 2
                        ps = bank_free(pe, i, (t, "den", ph))
                        pe.wait_ge(s_sum[h], 1 + i * NSUM + NSUM // 2 * t + (NT - 1) * (ph // 2 + 1))
                        for j in range(2):
                            last = nc.tensor.matmul(ps[j * HD:(j + 1) * HD, :], ones[:, :],
                                                    (psum_v, psum_g)[h][:, token_half(j)], start=True, stop=True)
                        last.then_inc(s_aux, 1)

                    for k in range(4):
                        qk_tile(0, k)
                    for k in range(32):
                        max_tile(0, k)
                    aux_read(pe, i, (t, "v", NT - 1))
                    neg_rows(0)
                    scores(0)
                    for g in range(TILES):
                        p, r = g // 16, g % 16
                        if r == 15 and p + 1 < PAIRS:
                            neg_rows(p + 1)
                        if g + 1 < TILES:
                            scores(g + 1)
                        for f in fillers(g):
                            (qk_tile if f[0] == "qk" else max_tile)(f[1], f[2])
                        prob_v(g)
                        if g % 8 == 1 and g > 8:
                            denominator(g // 8 - 1)
                    denominator(2 * PAIRS - 1)
                    pe.wait_ge(s_wvo, i * 64 + 32 * t + 32)
                    for k in range(8):
                        ps = bank_free(pe, i, (t, "o", k))
                        pe.wait_ge(s_olo, 1 + i * 16 + 8 * t + 7 + k // 4)
                        ct = k % 4
                        halves(ps[:, :], lambda a, c: w_vo[:, c // 2, a, c % 2, ct * P:(ct + 1) * P],
                               lambda b, c: o_t[:, b, c, token_half(k // 4)]).then_inc(s_aux, 1)


_INS = ["x", "L0_conv_w1", "L0_conv_b1", "L0_conv_w2", "L0_conv_b2",
        "L0_conv_hdn_w_qkv", "L0_conv_hdn_b_qkv", "L0_conv_hdn_w_o", "L0_conv_hdn_b_o",
        "L0_conv_eu_w_qkv", "L0_conv_eu_b_qkv", "L0_conv_eu_w_o", "L0_conv_eu_b_o"]
_OUTS = [((B, C, H, W), "float32")]


def kernel(**inputs):
    import numpy as _np
    import concourse.bacc as _bacc
    from concourse import mybir as _mybir
    from concourse.bass_utils import run_bass_kernel_spmd as _run

    nc = _bacc.Bacc("TRN2", target_bir_lowering=False, num_devices=1)
    arrays, args = {}, []
    for name in _INS:
        a = _np.ascontiguousarray(inputs[name])
        arrays[f"in_{name}_dram"] = a
        args.append(nc.dram_tensor(f"in_{name}_dram", a.shape, _mybir.dt.from_np(a.dtype), kind="ExternalInput").ap())
    for i, (shape, dtype) in enumerate(_OUTS):
        dt = _mybir.dt.from_np(_np.dtype(dtype))
        args.append(nc.dram_tensor(f"out_{i}_dram", shape, dt, kind="ExternalOutput").ap())
    build(nc, *args)
    r = _run(nc, [arrays], core_ids=[0])
    return r.results[0]["out_0_dram"]
```

```python
import numpy as np
import concourse.bass as bass
from concourse import mybir
from contextlib import ExitStack

F32 = mybir.dt.float32
F32R = mybir.dt.float32r
ALU = mybir.AluOpType
ACT = mybir.ActivationFunctionType
AX = mybir.AxisListType

B, C, H, W = 8, 512, 32, 32
N = H * W
P = 128
HALF = 512
KC = C // P
NT = N // P
HEADS, HD = 8, 64
PAIRS = HEADS // 2
HIDDEN = 128
GROUP = C // 32
SCALE = float(HD) ** -0.5
GN_EPS = 1e-5
EPS = 1e-5
SLOTS_P = 3
TILES = PAIRS * 2 * NT
ROWS = HALF // W

TANH_SERIES = [1.0, -1 / 3, 2 / 15, -17 / 315, 62 / 2835, -1382 / 155925, 21844 / 6081075]
TANH_BELOW = 0.1
ATANH_SERIES = [1.0, 1 / 3, 1 / 5, 1 / 7, 1 / 9, 1 / 11, 1 / 13]
ATANH_BELOW = 0.06

DVE_FIRST, DVE_STEPS = 38, 81
ACT_FIRST, ACT_STEPS = 4, 36

QK = [(0, 0), (1, 0), (1, 1), (0, 1)]

STATS, AGGREGATE, MEAN, VAR, RSTD_IN, RSTD, HIDDEN_AT, GATE_AT = 4, 12, 14, 17, 18, 19, 21, 23
NORMS, CLAMP, RNORM, NORM, EXP2N, SCALES, OPERAND = 24, 33, 34, 35, 36, 37, 38
STEPS_END = OPERAND + 9
GATE_TILES = {MEAN: "mean", VAR: "var", HIDDEN_AT: "hidden", GATE_AT: "gate"}
DEN = 2


def fillers(g):
    p, r = g // 16 + 1, g % 16
    if r < 4:
        return [("qk", p, r)]
    if r == 4 or r == 15:
        return []
    return [("max", p, k) for k in range(32 * (r - 5) // 10, 32 * (r - 4) // 10)]


def aux_tiles(t):
    if t < 0:
        out = [((t, GATE_TILES[g]), "D") for g in sorted(GATE_TILES)]
        out += [((t, "qk", PAIRS, k), "D") for k in range(4)]
        out += [((t, "max", PAIRS, k), "D") for k in range(32)]
        return out + [((t, "neg", PAIRS, h), "A") for h in range(2)]
    out = [((t, "v", m), "A") for m in range(NT)]
    for g in range(TILES):
        if g % 16 == 15:
            out += [((t, "neg", g // 16 + 1, h), "A") for h in range(2)]
        out += [((t,) + f, "D") for f in fillers(g)]
        if g % 8 == DEN and g > 8:
            out += [((t, "den", g // 8 - 1), "D")]
        if t == 1 and g in GATE_TILES:
            out += [((t, GATE_TILES[g]), "D")]
    out += [((t, "den", 2 * PAIRS - 1), "D")]
    return out + [((t, "o", k), "AD"[t]) for k in range(8)]


class Count:

    def __init__(self, sem, per, before=0):
        self.sem, self.per, self.before = sem, per, before

    def at(self, i, n):
        return 1 + n if i is None else i * self.per + (1 + self.before + n)


def build(nc, x, w1, b1, w2, b2, hw_qkv, hb_qkv, hw_o, hb_o, ew_qkv, eb_qkv, ew_o, eb_o, out):
    ctx = ExitStack()
    with ctx:
        ctx.enter_context(nc.allow_non_contiguous_dma(reason="biases, once"))

        def sb(name, shape, dt=F32):
            return ctx.enter_context(nc.sbuf_tensor(name, shape, dt))

        def pb(name, shape):
            return ctx.enter_context(nc.psum_tensor(name, shape, F32))

        x_v = x.rearrange("b (k p) h w -> b k p (h w)", p=P)
        out_v = out.rearrange("b (k p) h w -> b k p (h w)", p=P)
        w_split = nc.dram_tensor("w_split", (16, P, 2048), F32, kind="Internal").ap()

        w_qk = sb("w_qk", [P, 2, KC, 2, P], F32R)
        w_vo = sb("w_vo", [P, 2, 2, 2, C], F32R)
        xs = sb("xs", [P, 2, KC, N], F32R)
        qs = sb("qs", [P, 2, 2, N], F32R)
        qm = sb("qm", [P, 2, 2, N], F32R)
        kk = sb("kk", [P, 2, 2, N], F32R)
        kl = sb("kl", [P, 2, 2, N], F32R)
        v_y = sb("v_y", [P, NT, C])
        probs = sb("probs", [P, SLOTS_P, 2 * HALF])
        sums = [sb(f"sums{h}", [P, 2 * HALF]) for h in range(2)]
        o_t = sb("o_t", [P, 2, PAIRS, N], F32R)
        xin = sb("xin", [P, 2, HALF])
        res = sb("res", [P, 2, HALF])
        tmp = sb("tmp", [P, HALF])
        squares = sb("squares", [P, HALF])
        mxw = sb("mxw", [P, NT, 66], F32R)
        mxp = sb("mxp", [P, 2, NT, 2])
        ident = sb("ident", [P, P], F32R)
        group_mean = sb("group_mean", [P, P])
        ones = sb("ones", [P, HD])
        stats = sb("stats", [P, KC, 2, 6])
        mv = sb("mv", [P, KC, 2])
        gm = sb("gm", [P, KC])
        small = sb("small", [P, 8, KC])
        keep = sb("keep", [P, 2, KC])
        ss = sb("ss", [P, P])
        sc = sb("sc", [P, 4, P])
        bias_q = sb("bias_q", [P, 2, 3, KC])
        bias_o = sb("bias_o", [P, 2, KC])
        bias_1 = sb("bias_1", [P, 1])
        bias_2 = sb("bias_2", [P, KC])

        score_ps = [pb(f"score_ps{i}", [P, 2 * HALF]) for i in range(2)]
        acc_ps = [pb(f"acc_ps{i}", [P, HALF]) for i in range(2)]
        aux_ps = [pb(f"aux_ps{i}", [P, HALF]) for i in range(2)]

        FIRST, AUX = aux_tiles(-1), aux_tiles(0) + aux_tiles(1)
        assert len(FIRST) % 2 == 0 and len(AUX) % 2 == 0

        def frees(tiles, e, n=None):
            return sum(last == e for _, last in tiles[:n])

        at = {name: (tiles, n) for tiles in (FIRST, AUX) for n, (name, _) in enumerate(tiles)}

        def sem(name):
            return ctx.enter_context(nc.semaphore(name))

        def counted(name, per, before=0):
            return Count(sem(name), per, before)

        NSC = 2 * TILES
        NSUM = 2 * PAIRS * (NT - 1)
        s_const = sem("constants_set")
        s_ident = sem("identity_set")
        s_bias = sem("biases_loaded")
        s_raw = [sem(f"raw_weights_loaded{i}") for i in range(3)]
        s_split = sem("weights_split")
        s_wst = [sem(f"split_weights_stored{i}") for i in range(2)]
        c_wqk = counted("w_qk_loaded", 16 * 8, 16)
        c_wv = counted("w_v_loaded", 16 * 16)
        c_wo = counted("w_o_loaded", 16 * 4)
        c_xin = [counted(f"xin_loaded{i}", 16 * 17, 16 * 13) for i in range(2)]
        c_xfree = counted("xin_read", 32, 24)
        c_xg = counted("x_masked", 24, 16)
        c_xa = counted("x_squared_or_hi", 24, 16)
        c_pe_in = counted("gate_operand_made", 4, 4)
        c_d2a = counted("operand_of_scale_made", 3, 3)
        c_a2d = counted("function_of_scale_made", 3, 3)
        c_yd2a = counted("operand_of_y_scale_made", 2)
        c_ya2d = counted("function_of_y_scale_made", 2)
        c_aux = counted("aux_made", len(AUX), len(FIRST))
        c_free = {e: counted(n, frees(AUX, e), frees(FIRST, e))
                  for e, n in (("A", "aux_read_by_scalar"), ("D", "aux_read_by_vector"))}
        c_hi = counted("qk_hi_made", 128, 16)
        c_mx = counted("max_made", 16, 2)
        c_score = counted("scores_made", NSC)
        c_exp = counted("probs_made", NSC)
        c_pv = counted("probs_multiplied", NSC)
        c_sum = [counted(f"probs_summed{h}", NSUM) for h in range(2)]
        c_ln = counted("recip_guessed", 16)
        c_on = counted("o_normal", 16)
        c_ohi = counted("o_hi_made", 16)
        c_olo = counted("o_lo_made", 16)
        c_sq = counted("y_squared", 8)
        c_sqf = counted("y_square_read", 8)
        c_res = [counted(f"residual_loaded{i}", 128) for i in range(2)]
        c_fin = counted("result_made", 16)
        c_out = [counted(f"result_stored{i}", 128) for i in range(2)]
        c_dstep = counted("vector_step", DVE_STEPS, DVE_FIRST)
        c_astep = counted("scalar_step", ACT_STEPS, ACT_FIRST)
        COUNTS = [c_wqk, c_wv, c_wo, *c_xin, c_xfree, c_xg, c_xa, c_pe_in, c_d2a, c_a2d, c_yd2a, c_ya2d, c_aux,
                  *c_free.values(), c_hi, c_mx, c_score, c_exp, c_pv, *c_sum, c_ln, c_on, c_ohi, c_olo, c_sq,
                  c_sqf, *c_res, c_fin, *c_out, c_dstep, c_astep]

        def bank(name):
            return aux_ps[at[name][1] % 2]

        def aux_made(eng, i, name):
            eng.wait_ge(c_aux.sem, c_aux.at(i, at[name][1] + 1))
            return bank(name)

        def aux_read(eng, i, name):
            tiles, n = at[name]
            e = tiles[n][1]
            eng.wait_ge(c_free[e].sem, c_free[e].at(i, frees(tiles, e, n + 1)))

        def bank_free(pe, i, name):
            tiles, n = at[name]
            if n >= 2:
                aux_read(pe, i, tiles[n - 2][0])
            elif tiles is AUX:
                for e in "AD":
                    pe.wait_ge(c_free[e].sem, c_free[e].at(i, 0))
            return bank(name)

        SRCS = []
        for wq, wo in ((hw_qkv, hw_o), (ew_qkv, ew_o)):
            r, ro = (a.rearrange("(k p) n -> p k n", p=P) for a in (wq, wo))
            for p in range(PAIRS):
                SRCS.append([(r[:, :, j * C + p * P:j * C + (p + 1) * P], j) for j in range(2)])
            SRCS += [[(r[:, 2 * c:2 * c + 2, 2 * C:3 * C], None)] for c in range(2)]
            SRCS += [[(ro[:, 2 * c:2 * c + 2, :], None)] for c in range(2)]
        raw_at, count = [], [0] * 3
        for c, parts in enumerate(SRCS):
            count[c % 3] += 16 * len(parts)
            raw_at.append(count[c % 3])

        def token_half(h):
            return slice(h * HALF, (h + 1) * HALF)

        def x_chunk(j):
            return j // 2, token_half(j % 2)

        def new_image(t):
            return t != 0

        def before_stats(t):
            return 8 if t == 1 else 0

        def chunk_at(t, kind, j):
            if t == 0:
                return j, j
            b = before_stats(t)
            load = b + {"stats": 0, "w": 8, "norm": 10, "operand": 18}[kind] + j
            return load, load - (2 if kind in ("norm", "operand") else 0)

        def masked_at(t, kind, j):
            return j if t == 0 else before_stats(t) + (8 if kind == "operand" else 0) + j

        def owner(t, p):
            return (t, p) if p < PAIRS else ((t + 1) % 2, 0)

        def nth_pair(t, p):
            return 0 if t < 0 else PAIRS * t + p - 1

        block = ctx.enter_context(nc.Block())

        @block.sync
        def _(sp):
            for c in COUNTS:
                sp.sem_inc(c.sem, 1)
            for t, (bq, bo) in enumerate(((hb_qkv, hb_o), (eb_qkv, eb_o))):
                for j in range(3):
                    sp.dma_start(bias_q[:, t, j, :], bq[j * C:(j + 1) * C].rearrange("(k p) -> p k", p=P)).then_inc(s_bias, 16)
                sp.dma_start(bias_o[:, t, :], bo.rearrange("(k p) -> p k", p=P)).then_inc(s_bias, 16)
            sp.dma_start(bias_1[:, :], b1.rearrange("(p a) -> p a", a=1)).then_inc(s_bias, 16)
            sp.dma_start(bias_2[:, :], b2.rearrange("(k p) -> p k", p=P)).then_inc(s_bias, 16)

            def store_split(c):
                sp.wait_ge(s_split, 2 * c + 2)
                sp.dma_start(w_split[c], o_t[:, c % 2, 0:2, :].rearrange("p a n -> p (a n)").bitcast(F32)).then_inc(s_wst[c % 2], 16)

            for c, parts in enumerate(SRCS):
                if c >= 3:
                    sp.wait_ge(s_split, 2 * (c - 2))
                raw = probs[:, c % 3, :]
                for src, j in parts:
                    dst = (raw.rearrange("p (k n) -> p k n", k=2) if j is None
                           else raw.rearrange("p (k j n) -> p k j n", k=KC, j=2)[:, :, j, :])
                    sp.dma_start(dst, src).then_inc(s_raw[c % 3], 16)
                if c >= 2:
                    store_split(c - 2)
            store_split(14)
            store_split(15)

            def load_x(i, t, kind, j, src):
                n, freed = chunk_at(t, kind, j)
                if kind == "norm" and j < 2:
                    sp.wait_ge(c_aux.sem, c_aux.at(i, at[(t, ("hidden", "gate")[j])][1] + 1))
                elif n >= 2:
                    if kind in ("stats", "w") or t == 0:
                        sp.wait_ge(c_xfree.sem, c_xfree.at(i, n - 1))
                    else:
                        sp.wait_ge(c_xfree.sem, c_xfree.at(i, n - 3))
                elif i is not None:
                    sp.wait_ge(c_xfree.sem, c_xfree.at(i, 0))
                dst = xin[:, n % 2, :]
                sp.dma_start(dst.rearrange("p (k n) -> p k n", k=KC) if (kind, j) == ("w", 0) else dst,
                             src).then_inc(c_xin[n % 2].sem, 16)

            def load_chunks(i, t, kind, chunks, next_image=None):
                image = 0 if i is None else i if t == 0 else next_image
                for j in chunks:
                    k, cols = x_chunk(j)
                    load_x(i, t, kind, j, x_v[image, k, :, cols])

            def load_gate(i, t):
                load_x(i, t, "w", 0, w1.rearrange("(k p) n -> p k n", p=P))
                load_x(i, t, "w", 1, w2)

            def load_qk(t, p):
                t, p = owner(t, p)
                sp.dma_start(w_qk[:, :, :, :, :].rearrange("p a k j n -> p (a k j n)").bitcast(F32),
                             w_split[8 * t + p]).then_inc(c_wqk.sem, 16)

            load_chunks(None, -1, "stats", range(8))
            load_gate(None, -1)
            load_chunks(None, -1, "norm", range(8))
            load_chunks(None, -1, "operand", range(8))
            for q in s_wst:
                sp.wait_ge(q, 16 * 8)
            load_qk(-1, PAIRS)
            with sp.Fori(0, B) as i:
                next_image = sp.snap(sp.to_reg((i + 1) & (B - 1)))
                for t in range(2):
                    for ct in range(4):
                        if t:
                            sp.wait_ge(c_aux.sem, c_aux.at(i, at[(0, "o", 4 + ct)][1] + 1))
                        else:
                            sp.wait_ge(c_aux.sem, c_aux.at(i, ct - 3))
                        for c in range(2):
                            sp.dma_start(w_vo[:, c, :, :, ct * P:(ct + 1) * P].rearrange("p a k n -> p (a k) n").bitcast(F32),
                                         w_split[8 * t + 4 + c].rearrange("p (a n) -> p a n", a=4)[:, :, ct * P:(ct + 1) * P]
                                         ).then_inc(c_wv.sem, 16)
                    if t:
                        sp.wait_ge(c_aux.sem, c_aux.at(i, at[(0, "qk", PAIRS, 3)][1] + 1))
                    load_qk(t, 1)
                    sp.wait_ge(c_aux.sem, c_aux.at(i, at[(t, "v", NT - 1)][1] + 1))
                    for c in range(2):
                        sp.dma_start(w_vo[:, c, :, :, :].rearrange("p a k n -> p (a k n)").bitcast(F32),
                                     w_split[8 * t + 6 + c]).then_inc(c_wo.sem, 16)

                    def next_qk(p):
                        sp.wait_ge(c_aux.sem, c_aux.at(i, at[(t, "qk", p - 1, 3)][1] + 1))
                        load_qk(t, p)

                    next_qk(2)
                    if new_image(t):
                        load_chunks(i, t, "stats", range(8), next_image)
                        load_gate(i, t)
                    next_qk(3)
                    if new_image(t):
                        load_chunks(i, t, "norm", range(8), next_image)
                    load_chunks(i, t, "operand", range(2), next_image)
                    next_qk(4)
                    load_chunks(i, t, "operand", range(2, 8), next_image)

                    def tile_of(dram, k):
                        return dram[i, k % 4, :, token_half(k // 4)]

                    def store(k):
                        n = 8 * t + k
                        sp.wait_ge(c_fin.sem, c_fin.at(i, n + 1))
                        sp.dma_start(tile_of(out_v, k), res[:, n % 2, :]).then_inc(c_out[n % 2].sem, 16)

                    for k in range(8):
                        n = 8 * t + k
                        sp.wait_ge(c_out[n % 2].sem, c_out[n % 2].at(i, 16 * (n // 2)))
                        sp.dma_start(res[:, n % 2, :], tile_of((x_v, out_v)[t], k)).then_inc(c_res[n % 2].sem, 16)
                        if k >= 1:
                            store(k - 1)
                    store(7)
            for c in c_out:
                sp.wait_ge(c.sem, 1 + B * 128)

        @block.gpsimd
        def _(pool):
            pool.memset(tmp[:, 0:P], 0.0).then_inc(s_const, 1)
            pool.memset(group_mean[:, :], 1.0 / GROUP).then_inc(s_const, 1)
            pool.memset(ones[:, :], 1.0).then_inc(s_const, 1)
            pool.memset(mxw[:, :, :].bitcast(F32), 0.0).then_inc(s_const, 1)
            pool.memset(qm[:, :, :, :].bitcast(F32), 0.0).then_inc(s_const, 1)
            pool.memset(kl[:, :, :, :].bitcast(F32), 1.0).then_inc(s_const, 1)
            pool.wait_ge(s_const, 6)
            pool.affine_select(out=tmp[:, 0:P], in_=tmp[:, 0:P], compare_op=ALU.not_equal,
                               fill=1.0, base=0, pattern=[[-1, P]], channel_multiplier=1).then_inc(s_const, 1)
            g3 = group_mean[:, :].rearrange("p (g c) -> p g c", c=GROUP)
            pool.affine_select(out=g3, in_=g3, compare_op=ALU.is_ge, fill=0.0, base=0,
                               pattern=[[-GROUP, P // GROUP], [0, GROUP]], channel_multiplier=1).then_inc(s_const, 1)
            pool.wait_ge(s_const, 8)
            pool.affine_select(out=g3, in_=g3, compare_op=ALU.is_ge, fill=0.0, base=GROUP - 1,
                               pattern=[[GROUP, P // GROUP], [0, GROUP]], channel_multiplier=-1).then_inc(s_const, 1)
            with pool.Fori(0, B) as i:
                for t in range(2):
                    for ph in range(2 * PAIRS):
                        p, h = ph // 2, ph % 2
                        for m in range(1, NT):
                            g = TILES * t + 8 * ph + m
                            n = NSUM // 2 * t + (NT - 1) * p + m - 1
                            pool.wait_ge(c_exp.sem, c_exp.at(i, g + 1))
                            if m == 1 and p:
                                pool.wait_ge(c_aux.sem, c_aux.at(i, at[(t, "den", ph - 2)][1] + 1))
                            pool.wait_ge(c_sum[h].sem, c_sum[h].at(i, n))
                            a = probs[:, (g - 1) % SLOTS_P, :] if m == 1 else sums[h][:, :]
                            pool.tensor_tensor(sums[h][:, :], a, probs[:, g % SLOTS_P, :], ALU.add).then_inc(c_sum[h].sem, 1)

        @block.scalar
        def _(act):
            act.preload_act_table_set("natural_log_exp_and_others")
            act.wait_ge(s_bias, 16 * 10)
            act.wait_ge(s_ident, 1)
            steps = [0]

            def step(i, ins):
                steps[0] += 1
                ins.then_inc(c_astep.sem, 1)
                act.wait_ge(c_astep.sem, c_astep.at(i, steps[0]))

            def power(i, dst, src, e, made):
                step(i, act.activation(dst, src, ACT.Ln))
                act.activation(dst, dst, ACT.Exp, scale=e).then_inc(made.sem, 1)

            def operand_step(i, t, g):
                if new_image(t):
                    if g == RSTD_IN:
                        act.wait_ge(c_d2a.sem, c_d2a.at(i, 1))
                        power(i, small[:, 3, :], small[:, 2, :], -0.5, c_a2d)
                    if NORMS <= g < NORMS + 8:
                        j = g - NORMS
                        act.wait_ge(c_xg.sem, c_xg.at(i, masked_at(t, "norm", j) + 1))
                        if j:
                            act.wait_ge(c_xfree.sem, c_xfree.at(i, chunk_at(t, "norm", j)[1]))
                        elif i is not None:
                            act.wait_ge(c_sqf.sem, c_sqf.at(i, 8))
                        act.activation(squares[:, :], xin[:, j % 2, :], ACT.Square).then_inc(c_xa.sem, 1)
                    if g == RNORM:
                        act.wait_ge(c_d2a.sem, c_d2a.at(i, 2))
                        power(i, sc[:, 0, :], ss[:, :], -0.5, c_a2d)
                    if g == EXP2N:
                        act.wait_ge(c_d2a.sem, c_d2a.at(i, 3))
                        act.activation(sc[:, 2, :], sc[:, 1, :], ACT.Exp, scale=2.0).then_inc(c_a2d.sem, 1)
                if OPERAND <= g < OPERAND + 8:
                    j = g - OPERAND
                    k, cols = x_chunk(j)
                    act.wait_ge(c_xg.sem, c_xg.at(i, masked_at(t, "operand", j) + 1))
                    if j == 0 and i is not None:
                        act.wait_ge(c_aux.sem, c_aux.at(i, at[(t, "qk", PAIRS - 1, 3)][1] + 1))
                    act.activation(xs[:, 0, k, cols], xin[:, j % 2, :], ACT.Copy).then_inc(c_xa.sem, 1)

            def qk_hi(i, t, p, k):
                what, h = QK[k]
                ps = aux_made(act, i, (t, "qk", p, k))
                cols = token_half(h)
                tt, pp = owner(t, p)
                for j, (lo, hi) in enumerate(((0, HD), (HD, P))):
                    b = bias_q[lo:hi, tt, what, pp:pp + 1]
                    dsts = ((qs[lo:hi, p % 2, j, cols], qm[lo:hi, p % 2, j, cols]) if what == 0 else
                            (kk[0:HD, p % 2, j, cols], kk[HD:P, p % 2, j, cols]))
                    for d in dsts:
                        act.activation(d, ps[lo:hi, :], ACT.Identity, bias=b).then_inc(c_hi.sem, 1)

            def neg_rows(i, t, p):
                for h in range(2):
                    ps = aux_made(act, i, (t, "neg", p, h))
                    cols = token_half(h)
                    step(i, act.activation(qm[HD:HD + 1, p % 2, 0, cols], ps[HD:HD + 1, :], ACT.Copy))
                    act.activation(qm[0:1, p % 2, 1, cols], ps[0:1, :], ACT.Copy).then_inc(c_free["A"].sem, 1)

            for g in range(STEPS_END):
                operand_step(None, -1, g)
            for k in range(4):
                qk_hi(None, -1, PAIRS, k)
            neg_rows(None, -1, PAIRS)
            assert steps[0] == ACT_FIRST, ("ACT_FIRST", steps[0])
            steps[0] = 0
            with act.Fori(0, B) as i:
                for t in range(2):

                    def exps(g):
                        n = TILES * t + g
                        act.wait_ge(c_score.sem, c_score.at(i, n + 1))
                        last = max(n - SLOTS_P, -1)
                        act.wait_ge(c_pv.sem, c_pv.at(i, last + 1))
                        if last >= 0:
                            act.wait_ge(c_sum[(last // 8) % 2].sem, c_sum[(last // 8) % 2].at(i, (NT - 1) * (last // 16) + max(last % 8, 1)))
                        else:
                            act.wait_ge(c_sum[1].sem, c_sum[1].at(i, 0))
                        act.activation(probs[:, n % SLOTS_P, :], score_ps[n % 2][:, :], ACT.Exp,
                                       scale=SCALE).then_inc(c_exp.sem, 1)

                    def recip_guess(ph):
                        ps = aux_made(act, i, (t, "den", ph))
                        act.wait_ge(c_on.sem, c_on.at(i, 8 * t + ph))
                        power(i, tmp[:, :], ps[:, :], -1.0, c_ln)

                    def o_hi(ph):
                        p, h = ph // 2, ph % 2
                        act.wait_ge(c_on.sem, c_on.at(i, 8 * t + ph + 1))
                        act.activation(o_t[:, 0, p, token_half(h)], acc_ps[ph % 2][:, :],
                                       ACT.Identity, bias=bias_q[:, t, 2, p:p + 1]).then_inc(c_ohi.sem, 1)

                    exps(0)
                    for m in range(NT):
                        ps = aux_made(act, i, (t, "v", m))
                        if t:
                            act.wait_ge(c_fin.sem, c_fin.at(i, m + 1))
                        act.activation(v_y[:, m, :], ps[:, :], ACT.Copy).then_inc(c_free["A"].sem, 1)
                    for g in range(TILES):
                        p, r = g // 16, g % 16
                        if r == 15:
                            neg_rows(i, t, p + 1)
                        if g + 1 < TILES:
                            exps(g + 1)
                        for f in fillers(g):
                            if f[0] == "qk":
                                qk_hi(i, t, f[1], f[2])
                        if g % 8 == DEN and g > 8:
                            recip_guess(g // 8 - 1)
                        if g % 8 == DEN + 1 and g > 8:
                            o_hi(g // 8 - 1)
                        operand_step(i, t, g)
                    recip_guess(2 * PAIRS - 1)
                    o_hi(2 * PAIRS - 1)
                    if t == 0:
                        for k in range(8):
                            ps = aux_made(act, i, (0, "o", k))
                            act.activation(v_y[:, k, :], ps[:, :], ACT.Identity,
                                           bias=bias_o[:, 0, k % 4:k % 4 + 1]).then_inc(c_free["A"].sem, 1)
                            aux_read(act, i, (0, "o", k))
                            if k:
                                act.wait_ge(c_sqf.sem, c_sqf.at(i, k))
                            else:
                                act.wait_ge(c_xfree.sem, c_xfree.at(i, 0))
                            act.activation(squares[:, :], v_y[:, k, :], ACT.Square).then_inc(c_sq.sem, 1)
                        act.wait_ge(c_yd2a.sem, c_yd2a.at(i, 1))
                        power(i, sc[:, 0, :], ss[:, :], -0.5, c_ya2d)
                        act.wait_ge(c_yd2a.sem, c_yd2a.at(i, 2))
                        step(i, act.activation(sc[:, 2, :], sc[:, 1, :], ACT.Ln, bias=1.0))
                        act.activation(sc[:, 3, :], sc[:, 1, :], ACT.Ln, bias=1.0, scale=-1.0).then_inc(c_ya2d.sem, 1)
                assert steps[0] == ACT_STEPS, ("ACT_STEPS", steps[0])

        @block.vector
        def _(dve):
            for c in range(len(SRCS)):
                dve.wait_ge(s_raw[c % 3], raw_at[c])
                if c >= 2:
                    dve.wait_ge(s_wst[c % 2], 16 * (c // 2))
                dve.tensor_copy(o_t[:, c % 2, 0, :], probs[:, c % 3, :]).then_inc(s_split, 1)
                dve.wait_ge(s_split, 2 * c + 1)
                dve.tensor_tensor(o_t[:, c % 2, 1, :], probs[:, c % 3, :], o_t[:, c % 2, 0, :].bitcast(F32),
                                  ALU.subtract).then_inc(s_split, 1)
            dve.wait_ge(s_const, 9)
            dve.tensor_copy(ident[:, :], tmp[:, 0:P]).then_inc(s_ident, 1)
            dve.wait_ge(s_ident, 1)
            dve.wait_ge(s_bias, 16 * 10)
            steps = [0]

            def step(i, ins):
                steps[0] += 1
                ins.then_inc(c_dstep.sem, 1)
                dve.wait_ge(c_dstep.sem, c_dstep.at(i, steps[0]))

            def newton_rsqrt(i, r, v, work):
                step(i, dve.tensor_tensor(work, r, r, ALU.mult))
                step(i, dve.tensor_tensor(work, work, v, ALU.mult))
                step(i, dve.scalar_tensor_tensor(work, work, 3.0, r, ALU.subtract, ALU.mult))
                step(i, dve.tensor_scalar(r, work, -0.5, None, ALU.mult))

            def series(i, dst, s, coefs):
                step(i, dve.tensor_scalar(dst, s, coefs[-1], None, ALU.mult))
                for c in coefs[-2:0:-1]:
                    step(i, dve.scalar_tensor_tensor(dst, dst, c, s, ALU.add, ALU.mult))
                step(i, dve.tensor_scalar(dst, dst, coefs[0], None, ALU.add))

            def blend(i, dst, small_one, s, below):
                step(i, dve.tensor_scalar(s, s, below, None, ALU.is_lt))
                step(i, dve.tensor_tensor(small_one, small_one, dst, ALU.subtract))
                step(i, dve.tensor_tensor(small_one, small_one, s, ALU.mult))
                step(i, dve.tensor_tensor(dst, dst, small_one, ALU.add))

            def rows(ap):
                return ap.rearrange("p (r w) -> p r w", w=W)

            def per_row(a, k0):
                return sc[:, a, k0:k0 + ROWS].unsqueeze(2).to_broadcast([P, ROWS, W])

            def chunk_in(i, t, kind, j):
                n = chunk_at(t, kind, j)[0]
                dve.wait_ge(c_xin[n % 2].sem, c_xin[n % 2].at(i, 16 * (n // 2 + 1)))
                return xin[:, n % 2, :]

            def operand_step(i, t, g):
                if new_image(t):
                    if STATS <= g < STATS + 8:
                        j = g - STATS
                        dve.bn_stats(stats[:, j // 2, j % 2, :], chunk_in(i, t, "stats", j)).then_inc(c_xfree.sem, 1)
                    if g == AGGREGATE:
                        dve.wait_ge(c_xfree.sem, c_xfree.at(i, chunk_at(t, "stats", 7)[1] + 1))
                        dve.memset(small[:, 7, :], 0.0)
                        for k in range(KC):
                            last = dve.bn_aggr(mv[:, k, :], stats[:, k, :, :].rearrange("p h s -> p (h s)"))
                        last.then_inc(c_pe_in.sem, 1)
                    if g == MEAN:
                        ps = aux_made(dve, i, (t, "mean"))
                        dve.tensor_copy(gm[:, :], ps[:, 0:KC]).then_inc(c_free["D"].sem, 1)
                        aux_read(dve, i, (t, "mean"))
                        step(i, dve.tensor_tensor(small[:, 1, :], mv[:, :, 0], gm[:, :], ALU.subtract))
                        step(i, dve.tensor_tensor(small[:, 0, :], small[:, 1, :], small[:, 1, :], ALU.mult))
                        dve.tensor_tensor(small[:, 0, :], small[:, 0, :], mv[:, :, 1], ALU.add).then_inc(c_pe_in.sem, 1)
                    if g == VAR:
                        ps = aux_made(dve, i, (t, "var"))
                        dve.tensor_scalar(small[:, 2, :], ps[:, 0:KC], GN_EPS, None, ALU.add).then_inc(c_free["D"].sem, 1)
                        aux_read(dve, i, (t, "var"))
                        dve.tensor_copy(small[:, 6, :], small[:, 2, :]).then_inc(c_d2a.sem, 1)
                    if g == RSTD:
                        dve.wait_ge(c_a2d.sem, c_a2d.at(i, 1))
                        newton_rsqrt(i, small[:, 3, :], small[:, 2, :], small[:, 4, :])
                        dve.tensor_tensor(small[:, 0, :], small[:, 1, :], small[:, 3, :], ALU.mult).then_inc(c_pe_in.sem, 1)
                    if g == HIDDEN_AT:
                        ps = aux_made(dve, i, (t, "hidden"))
                        dve.tensor_scalar(small[:, 4, 0:1], ps[:, 0:1], bias_1[:, 0:1], None, ALU.add).then_inc(c_free["D"].sem, 1)
                        aux_read(dve, i, (t, "hidden"))
                        dve.tensor_scalar(small[:, 5, 0:1], small[:, 4, 0:1], 0.0, None, ALU.max).then_inc(c_pe_in.sem, 1)
                    if g == GATE_AT:
                        ps = aux_made(dve, i, (t, "gate"))
                        dve.tensor_tensor(small[:, 4, :], ps[:, 0:KC], bias_2[:, :], ALU.add).then_inc(c_free["D"].sem, 1)
                        aux_read(dve, i, (t, "gate"))
                        step(i, dve.tensor_scalar(small[:, 5, :], small[:, 4, :], 0.0, None, ALU.is_gt))
                        step(i, dve.tensor_tensor(keep[:, 0, :], small[:, 3, :], small[:, 5, :], ALU.mult))
                        step(i, dve.tensor_tensor(keep[:, 1, :], small[:, 3, :], keep[:, 0, :], ALU.subtract))
                    if NORMS < g <= NORMS + 8:
                        j = g - NORMS - 1
                        dve.wait_ge(c_xa.sem, c_xa.at(i, masked_at(t, "norm", j) + 1))
                        dve.tensor_reduce(ss[:, j * ROWS:(j + 1) * ROWS], rows(squares[:, :]), AX.X,
                                          ALU.add).then_inc(c_xfree.sem, 1)
                    if NORMS <= g < NORMS + 8:
                        j = g - NORMS
                        k = j // 2
                        chunk = chunk_in(i, t, "norm", j)
                        dve.tensor_scalar(chunk, chunk, gm[:, k:k + 1], keep[:, 0, k:k + 1],
                                          ALU.subtract, ALU.mult).then_inc(c_xg.sem, 1)
                    if g == CLAMP:
                        dve.wait_ge(c_xfree.sem, c_xfree.at(i, chunk_at(t, "norm", 7)[1] + 1))
                        dve.tensor_scalar(ss[:, :], ss[:, :], 2.0 ** -60, None, ALU.max).then_inc(c_d2a.sem, 1)
                    if g == NORM:
                        dve.wait_ge(c_a2d.sem, c_a2d.at(i, 2))
                        newton_rsqrt(i, sc[:, 0, :], ss[:, :], sc[:, 1, :])
                        step(i, dve.tensor_tensor(sc[:, 1, :], ss[:, :], sc[:, 0, :], ALU.mult))
                        dve.tensor_scalar(sc[:, 1, :], sc[:, 1, :], 20.0, None, ALU.min).then_inc(c_d2a.sem, 1)
                    if g == SCALES:
                        dve.wait_ge(c_a2d.sem, c_a2d.at(i, 3))
                        step(i, dve.tensor_scalar(sc[:, 2, :], sc[:, 2, :], 1.0, None, ALU.add))
                        step(i, dve.reciprocal(sc[:, 3, :], sc[:, 2, :]))
                        step(i, dve.tensor_scalar(sc[:, 3, :], sc[:, 3, :], -2.0, 1.0, ALU.mult, ALU.add))
                        step(i, dve.tensor_tensor(sc[:, 3, :], sc[:, 3, :], sc[:, 0, :], ALU.mult))
                        step(i, dve.tensor_scalar(ss[:, :], ss[:, :], 1.0, None, ALU.min))
                        series(i, sc[:, 1, :], ss[:, :], TANH_SERIES)
                        blend(i, sc[:, 3, :], sc[:, 1, :], ss[:, :], TANH_BELOW)
                if OPERAND < g <= OPERAND + 8:
                    j = g - OPERAND - 1
                    k, cols = x_chunk(j)
                    dve.wait_ge(c_xa.sem, c_xa.at(i, masked_at(t, "operand", j) + 1))
                    dve.tensor_tensor(xs[:, 1, k, cols], xin[:, j % 2, :], xs[:, 0, k, cols].bitcast(F32),
                                      ALU.subtract).then_inc(c_xfree.sem, 1)
                if OPERAND <= g < OPERAND + 8:
                    j = g - OPERAND
                    k = j // 2
                    chunk = chunk_in(i, t, "operand", j)
                    hyperbolic = new_image(t)
                    scale = keep[:, 0 if hyperbolic else 1, k:k + 1]
                    norm = dve.tensor_scalar(chunk, chunk, gm[:, k:k + 1], scale, ALU.subtract, ALU.mult)
                    if hyperbolic:
                        step(i, norm)
                        dve.tensor_tensor(rows(chunk), rows(chunk), per_row(3, j * ROWS), ALU.mult).then_inc(c_xg.sem, 1)
                    else:
                        norm.then_inc(c_xg.sem, 1)

            def qk_lo(i, t, p, k):
                what, h = QK[k]
                ps = aux_made(dve, i, (t, "qk", p, k))
                dve.wait_ge(c_hi.sem, c_hi.at(i, 4 * (4 * nth_pair(t, p) + k + 1)))
                cols = token_half(h)
                tt, pp = owner(t, p)
                for j, (lo, hi) in enumerate(((0, HD), (HD, P))):
                    high = (qs, kk)[what][lo:hi, p % 2, j, cols].bitcast(F32)
                    dst = qs[P - hi:P - lo, p % 2, j, cols] if what == 0 else kl[lo:hi, p % 2, j, cols]
                    ins = dve.scalar_tensor_tensor(dst, ps[lo:hi, :], bias_q[lo:hi, tt, what, pp:pp + 1], high,
                                                   ALU.add, ALU.subtract)
                ins.then_inc(c_free["D"].sem, 1)

            def max_tile(i, t, p, k):
                j, n, h = k // 16, (k // 2) % 8, k % 2
                ps = aux_made(dve, i, (t, "max", p, k))
                if k == 0 and i is not None:
                    dve.wait_ge(c_mx.sem, c_mx.at(i, 2 * nth_pair(t, p)))
                dve.tensor_reduce(mxp[:, j, n, h:h + 1], ps[:, :], AX.X, ALU.max).then_inc(c_free["D"].sem, 1)

            def combine(i, t, p):
                aux_read(dve, i, (t, "max", p, 31))
                for j in range(2):
                    dve.tensor_reduce(mxw[:, :, HD * (1 - j)], mxp[:, j, :, :], AX.X, ALU.max,
                                      negate=True).then_inc(c_mx.sem, 1)

            for g in range(STEPS_END):
                operand_step(None, -1, g)
            for k in range(4):
                qk_lo(None, -1, PAIRS, k)
            for k in range(32):
                max_tile(None, -1, PAIRS, k)
            combine(None, -1, PAIRS)
            assert steps[0] == DVE_FIRST, ("DVE_FIRST", steps[0])
            steps[0] = 0
            with dve.Fori(0, B) as i:
                for t in range(2):

                    def normalise(ph):
                        ps = aux_made(dve, i, (t, "den", ph))
                        dve.wait_ge(c_ln.sem, c_ln.at(i, 8 * t + ph + 1))
                        step(i, dve.tensor_tensor(ps[:, :], ps[:, :], tmp[:, :], ALU.mult))
                        dve.scalar_tensor_tensor(tmp[:, :], ps[:, :], 2.0, tmp[:, :], ALU.subtract,
                                                 ALU.mult).then_inc(c_free["D"].sem, 1)
                        aux_read(dve, i, (t, "den", ph))
                        acc = acc_ps[ph % 2]
                        dve.scalar_tensor_tensor(acc[:, :], acc[:, :], -1.0, tmp[:, :], ALU.mult,
                                                 ALU.mult).then_inc(c_on.sem, 1)

                    def o_lo(ph):
                        p, h = ph // 2, ph % 2
                        dve.wait_ge(c_ohi.sem, c_ohi.at(i, 8 * t + ph + 1))
                        dve.scalar_tensor_tensor(o_t[:, 1, p, token_half(h)], acc_ps[ph % 2][:, :],
                                                 bias_q[:, t, 2, p:p + 1], o_t[:, 0, p, token_half(h)].bitcast(F32),
                                                 ALU.add, ALU.subtract).then_inc(c_olo.sem, 1)

                    for g in range(TILES):
                        p, r = g // 16, g % 16
                        for f in fillers(g):
                            (qk_lo if f[0] == "qk" else max_tile)(i, t, f[1], f[2])
                        if r == 14:
                            combine(i, t, p + 1)
                        if g % 8 == DEN and g > 8:
                            normalise(g // 8 - 1)
                        if g % 8 == DEN + 2 and g > 8:
                            o_lo(g // 8 - 1)
                        operand_step(i, t, g)
                    normalise(2 * PAIRS - 1)
                    o_lo(2 * PAIRS - 1)
                    if t == 0:
                        for k in range(8):
                            dve.wait_ge(c_sq.sem, c_sq.at(i, k + 1))
                            dve.tensor_reduce(ss[:, k * ROWS:(k + 1) * ROWS], rows(squares[:, :]), AX.X,
                                              ALU.add).then_inc(c_sqf.sem, 1)
                        dve.wait_ge(c_sqf.sem, c_sqf.at(i, 8))
                        dve.tensor_scalar(ss[:, :], ss[:, :], 2.0 ** -60, None, ALU.max).then_inc(c_yd2a.sem, 1)
                        dve.wait_ge(c_ya2d.sem, c_ya2d.at(i, 1))
                        newton_rsqrt(i, sc[:, 0, :], ss[:, :], sc[:, 1, :])
                        step(i, dve.tensor_tensor(sc[:, 1, :], ss[:, :], sc[:, 0, :], ALU.mult))
                        dve.tensor_scalar(sc[:, 1, :], sc[:, 1, :], float(np.float32(1.0) - np.float32(EPS)), None,
                                          ALU.min).then_inc(c_yd2a.sem, 1)
                        dve.wait_ge(c_ya2d.sem, c_ya2d.at(i, 2))
                        step(i, dve.tensor_tensor(sc[:, 3, :], sc[:, 2, :], sc[:, 3, :], ALU.subtract))
                        step(i, dve.scalar_tensor_tensor(sc[:, 3, :], sc[:, 3, :], 0.5, sc[:, 0, :], ALU.mult, ALU.mult))
                        step(i, dve.tensor_scalar(ss[:, :], ss[:, :], 1.0, None, ALU.min))
                        series(i, sc[:, 1, :], ss[:, :], ATANH_SERIES)
                        blend(i, sc[:, 3, :], sc[:, 1, :], ss[:, :], ATANH_BELOW)
                        for k in range(8):
                            y = v_y[:, k, :]
                            step(i, dve.tensor_tensor(rows(y), rows(y), per_row(3, k * ROWS), ALU.mult))
                            dve.wait_ge(c_res[k % 2].sem, c_res[k % 2].at(i, 16 * (k // 2 + 1)))
                            dve.tensor_tensor(res[:, k % 2, :], res[:, k % 2, :], y, ALU.add).then_inc(c_fin.sem, 1)
                    else:
                        for k in range(8):
                            ps = aux_made(dve, i, (1, "o", k))
                            dve.wait_ge(c_res[k % 2].sem, c_res[k % 2].at(i, 64 + 16 * (k // 2 + 1)))
                            r = res[:, k % 2, :]
                            dve.scalar_tensor_tensor(r, ps[:, :], bias_o[:, 1, k % 4:k % 4 + 1], r,
                                                     ALU.add, ALU.add).then_inc(c_free["D"].sem, 1)
                            aux_read(dve, i, (1, "o", k))
                            dve.tensor_copy(small[:, 7, 0:1], small[:, 6, 0:1]).then_inc(c_fin.sem, 1)
                assert steps[0] == DVE_STEPS, ("DVE_STEPS", steps[0])

        @block.tensor
        def _(pe):
            pe.wait_ge(s_const, 9)
            pe.wait_ge(s_ident, 1)

            def halves(ps, lhs, rhs):
                todo = [(k, a, b) for k in range(KC) for a, b in ((0, 0), (0, 1), (1, 0))]
                for n, (k, a, b) in enumerate(todo):
                    last = nc.tensor.matmul(ps, lhs(a, k), rhs(b, k), start=(n == 0), stop=(n == len(todo) - 1))
                return last

            def gate_tile(i, t, g):
                name = GATE_TILES[g]
                ps = bank_free(pe, i, (t, name))
                pe.wait_ge(c_pe_in.sem, c_pe_in.at(i, sorted(GATE_TILES).index(g) + 1))
                if name == "mean":
                    nc.tensor.matmul(ps[:, 0:KC], group_mean[:, :], mv[:, :, 0], start=True, stop=True).then_inc(c_aux.sem, 1)
                if name == "var":
                    nc.tensor.matmul(ps[:, 0:KC], group_mean[:, :], small[:, 0, :], start=True, stop=True).then_inc(c_aux.sem, 1)
                w = {"hidden": 0, "gate": 1}.get(name)
                if w is not None:
                    n = chunk_at(t, "w", w)[0]
                    pe.wait_ge(c_xin[n % 2].sem, c_xin[n % 2].at(i, 16 * (n // 2 + 1)))
                    for k in range(KC):
                        if w == 0:
                            last = nc.tensor.matmul(ps[:, 0:1], xin[:, n % 2, k * HIDDEN:(k + 1) * HIDDEN],
                                                    small[:, 0, k:k + 1], start=(k == 0), stop=(k == KC - 1))
                        else:
                            last = nc.tensor.matmul(ps[:, k:k + 1], xin[:, n % 2, k * P:(k + 1) * P], small[:, 5, 0:1],
                                                    start=True, stop=True)
                    last.then_inc(c_aux.sem, 1)

            def qk_tile(i, t, p, k):
                what, h = QK[k]
                ps = bank_free(pe, i, (t, "qk", p, k))
                if k == 0:
                    pe.wait_ge(c_wqk.sem, c_wqk.at(i, 16 * (nth_pair(t, p) + 1)))
                    if p == PAIRS:
                        pe.wait_ge(c_xfree.sem, c_xfree.at(i, chunk_at(t, "operand", 7)[1] + 1))
                halves(ps[:, :], lambda a, c: w_qk[:, a, c, what, :],
                       lambda b, c: xs[:, b, c, token_half(h)]).then_inc(c_aux.sem, 1)

            def max_tile(i, t, p, k):
                j, n, h = k // 16, (k // 2) % 8, k % 2
                ps = bank_free(pe, i, (t, "max", p, k))
                if k == 0:
                    aux_read(pe, i, (t, "qk", p, 3))
                nc.tensor.matmul(ps[:, :], qs[:, p % 2, j, n * P:(n + 1) * P], kk[:, p % 2, j, token_half(h)],
                                 start=True, stop=True).then_inc(c_aux.sem, 1)

            def neg_rows(i, t, p):
                pe.wait_ge(c_mx.sem, c_mx.at(i, 2 * (nth_pair(t, p) + 1)))
                for h in range(2):
                    ps = bank_free(pe, i, (t, "neg", p, h))
                    for n in range(4):
                        last = nc.tensor.matmul(ps[0:HD + 1, n * P:(n + 1) * P], mxw[:, 4 * h + n, 0:HD + 1],
                                                ident[:, :], start=True, stop=True)
                    last.then_inc(c_aux.sem, 1)

            for g in sorted(GATE_TILES):
                gate_tile(None, -1, g)
            for k in range(4):
                qk_tile(None, -1, PAIRS, k)
            for k in range(32):
                max_tile(None, -1, PAIRS, k)
            neg_rows(None, -1, PAIRS)
            with pe.Fori(0, B) as i:
                for t in range(2):

                    def scores(g, j):
                        p, h, m = g // 16, (g // 8) % 2, g % 8
                        n = TILES * t + g
                        if g % 16 == 0 and j == 0:
                            if g:
                                aux_read(pe, i, (t, "neg", p, 1))
                            elif t:
                                aux_read(pe, i, (0, "neg", PAIRS, 1))
                            else:
                                pe.wait_ge(c_free["A"].sem, c_free["A"].at(i, 0))
                        if j == 0:
                            pe.wait_ge(c_exp.sem, c_exp.at(i, max(n - 1, 0)))
                        o = score_ps[n % 2][:, token_half(j)]
                        nc.tensor.matmul(o, kk[:, p % 2, j, m * P:(m + 1) * P], qs[:, p % 2, j, token_half(h)],
                                         start=True, stop=False)
                        last = nc.tensor.matmul(o, kl[:, p % 2, j, m * P:(m + 1) * P], qm[:, p % 2, j, token_half(h)],
                                                start=False, stop=True)
                        if j:
                            last.then_inc(c_score.sem, 1)

                    def prob_v(g):
                        p, ph, m = g // 16, g // 8, g % 8
                        n = TILES * t + g
                        pe.wait_ge(c_exp.sem, c_exp.at(i, n + 1))
                        if g == 0:
                            aux_read(pe, i, (t, "v", NT - 1))
                        if m == 0:
                            pe.wait_ge(c_olo.sem, c_olo.at(i, max(8 * t + ph - 1, 0)))
                        for j in range(2):
                            head = slice((2 * p + j) * HD, (2 * p + j + 1) * HD)
                            last = nc.tensor.matmul(acc_ps[ph % 2][j * HD:(j + 1) * HD, :], v_y[:, m, head],
                                                    probs[:, n % SLOTS_P, token_half(j)],
                                                    start=(m == 0), stop=(m == NT - 1))
                        last.then_inc(c_pv.sem, 1)

                    def denominator(ph):
                        h = ph % 2
                        ps = bank_free(pe, i, (t, "den", ph))
                        pe.wait_ge(c_sum[h].sem, c_sum[h].at(i, NSUM // 2 * t + (NT - 1) * (ph // 2 + 1)))
                        for j in range(2):
                            last = nc.tensor.matmul(ps[j * HD:(j + 1) * HD, :], ones[:, :], sums[h][:, token_half(j)],
                                                    start=True, stop=True)
                        last.then_inc(c_aux.sem, 1)

                    scores(0, 0)
                    scores(0, 1)
                    pe.wait_ge(c_wv.sem, c_wv.at(i, 16 * 8 * (t + 1)))
                    for m in range(NT):
                        ps = bank_free(pe, i, (t, "v", m))
                        halves(ps[:, :], lambda a, k: xs[:, a, k, m * P:(m + 1) * P],
                               lambda b, k: w_vo[:, k // 2, b, k % 2, :]).then_inc(c_aux.sem, 1)
                    for g in range(TILES):
                        p, r = g // 16, g % 16

                        def fill(todo):
                            for f in todo:
                                (qk_tile if f[0] == "qk" else max_tile)(i, t, f[1], f[2])

                        todo = fillers(g)
                        if r == 15:
                            neg_rows(i, t, p + 1)
                            prob_v(g)
                        if g + 1 < TILES:
                            scores(g + 1, 0)
                            fill(todo[0:1])
                            scores(g + 1, 1)
                            fill(todo[1:2])
                        if r != 15:
                            prob_v(g)
                        fill(todo[2:])
                        if g % 8 == DEN and g > 8:
                            denominator(g // 8 - 1)
                        if t == 1 and g in GATE_TILES:
                            gate_tile(i, t, g)
                    denominator(2 * PAIRS - 1)
                    pe.wait_ge(c_wo.sem, c_wo.at(i, 32 * (t + 1)))
                    for k in range(8):
                        ps = bank_free(pe, i, (t, "o", k))
                        pe.wait_ge(c_olo.sem, c_olo.at(i, 8 * t + 7 + k // 4))
                        ct = k % 4
                        halves(ps[:, :], lambda a, c: w_vo[:, c // 2, a, c % 2, ct * P:(ct + 1) * P],
                               lambda b, c: o_t[:, b, c, token_half(k // 4)]).then_inc(c_aux.sem, 1)


_INS = ["x", "L0_conv_w1", "L0_conv_b1", "L0_conv_w2", "L0_conv_b2",
        "L0_conv_hdn_w_qkv", "L0_conv_hdn_b_qkv", "L0_conv_hdn_w_o", "L0_conv_hdn_b_o",
        "L0_conv_eu_w_qkv", "L0_conv_eu_b_qkv", "L0_conv_eu_w_o", "L0_conv_eu_b_o"]
_OUTS = [((B, C, H, W), "float32")]


def kernel(**inputs):
    import numpy as _np
    import concourse.bacc as _bacc
    from concourse import mybir as _mybir
    from concourse.bass_utils import run_bass_kernel_spmd as _run

    nc = _bacc.Bacc("TRN2", target_bir_lowering=False, num_devices=1)
    arrays, args = {}, []
    for name in _INS:
        a = _np.ascontiguousarray(inputs[name])
        arrays[f"in_{name}_dram"] = a
        args.append(nc.dram_tensor(f"in_{name}_dram", a.shape, _mybir.dt.from_np(a.dtype), kind="ExternalInput").ap())
    for i, (shape, dtype) in enumerate(_OUTS):
        dt = _mybir.dt.from_np(_np.dtype(dtype))
        args.append(nc.dram_tensor(f"out_{i}_dram", shape, dt, kind="ExternalOutput").ap())
    build(nc, *args)
    r = _run(nc, [arrays], core_ids=[0])
    return r.results[0]["out_0_dram"]
```

```python
import numpy as np
import concourse.bass as bass
from concourse import mybir
from contextlib import ExitStack

F32 = mybir.dt.float32
F32R = mybir.dt.float32r
ALU = mybir.AluOpType
ACT = mybir.ActivationFunctionType
AX = mybir.AxisListType

B, C, H, W = 8, 512, 32, 32
N = H * W
P = 128
HALF = 512
KC = C // P
NT = N // P
HEADS, HD = 8, 64
PAIRS = HEADS // 2
HIDDEN = 128
GROUP = C // 32
SCALE = float(HD) ** -0.5
GN_EPS = 1e-5
EPS = 1e-5
SLOTS_P = 3
SCORE_BANKS, AUX_BANKS = 3, 3
XIN = 3
TILES = PAIRS * 2 * NT
ROWS = HALF // W

TANH_SERIES = [1.0, -1 / 3, 2 / 15, -17 / 315, 62 / 2835, -1382 / 155925, 21844 / 6081075]
TANH_BELOW = 0.1
ATANH_SERIES = [1.0, 1 / 3, 1 / 5, 1 / 7, 1 / 9, 1 / 11, 1 / 13]
ATANH_BELOW = 0.06

DVE_FIRST, DVE_STEPS = 30, 73
ACT_FIRST, ACT_STEPS = 4, 36

QK = [(0, 0), (1, 0), (1, 1), (0, 1)]

STATS, AGGREGATE, MEAN, VAR, RSTD_IN, RSTD, HIDDEN_AT, GATE_AT = 7, 15, 16, 17, 18, 19, 20, 22
NORMS, CLAMP, RNORM, NORM, EXP2N, SCALES, OPERAND = 23, 32, 33, 34, 35, 36, 37
STEPS_END = OPERAND + 9
Y_RNORM, Y_NORM, Y_LOGS, Y_SCALE = 0, 2, 3, 5
Y_SUM = 58
GATE_TILES = {MEAN: "mean", VAR: "var", HIDDEN_AT: "hidden", GATE_AT: "gate"}
DENS = {8 * ph + (13 if ph % 2 else 11): ph for ph in range(2 * PAIRS - 1)}

MAXES = [[2, 2, 2, 2, 2, 3, 2, 3, 2, 3, 3, 3, 3, 0, 0, 0],
         [0, 3, 3, 3, 3, 3, 3, 2, 3, 3, 2, 2, 2, 0, 0, 0]]
QK_AT = [-2, -1, 1, 3]
MAX_ORDER = [(j, n, h) for h in range(2) for n in range(4) for j in range(2)]
MAX_ORDER += [(j, n, h) for h in range(2) for n in range(4, 8) for j in range(2)]
COMBINE, NEG = 13, 14


def maxes(g):
    p, r = g // 16, g % 16
    counts = MAXES[min(p, 1)]
    return [("max", p + 1, k) for k in range(sum(counts[:r]), sum(counts[:r + 1]))]


def projection(g):
    if g < NT - 1:
        return [("v", g + 1)]
    return [("qk", q, k) for q in range(2, PAIRS + 1) for k in range(4) if g == 16 * (q - 1) + QK_AT[k]]


def aux_tiles(t):
    if t < 0:
        out = [((t, GATE_TILES[g]), "D", -1) for g in sorted(GATE_TILES)]
        out += [((t, "qk", PAIRS, k), "Q", -1) for k in range(4)]
        out += [((t, "max", PAIRS, k), "D", -1) for k in range(32)]
        return out + [((t, "neg", PAIRS, h), "A", -1) for h in range(2)]
    reader = {"v": "A", "qk": "Q", "max": "D"}
    out = [((t, "qk", 1, k), "Q", -1) for k in range(4)] + [((t, "v", 0), "A", -1)]
    for g in range(TILES):
        todo = maxes(g)
        out += [((t,) + f, reader[f[0]], g) for f in todo[:1]]
        if g % 16 == NEG:
            out += [((t, "neg", g // 16 + 1, h), "A", g) for h in range(2)]
        out += [((t,) + f, reader[f[0]], g) for f in projection(g) + todo[1:]]
        if g in DENS:
            out += [((t, "den", DENS[g]), "N", g)]
        if t == 1 and g in GATE_TILES:
            out += [((t, GATE_TILES[g]), "D", g)]
    out += [((t, "o", 0), "AD"[t], TILES), ((t, "den", 2 * PAIRS - 1), "N", TILES)]
    return out + [((t, "o", k), "AD"[t], TILES) for k in range(1, 8)]


def banks(tiles):
    last, out = [None] * AUX_BANKS, []
    for n, (name, reader, g) in enumerate(tiles):
        first = n == 0 or tiles[n - 1][2] != g

        def age(b):
            (block, *_), e, group = tiles[last[b]] if last[b] is not None else ((None,), "", -1)
            late = e in "QN" and block == name[0] and 0 <= group and g < TILES
            return g - group if late else 9

        sure = [b for b in range(AUX_BANKS) if age(b) > (2 if first else 1)]
        b = min(sure or [b for b in range(AUX_BANKS) if age(b) > 1], key=lambda b: -1 if last[b] is None else last[b])
        out.append((b, last[b]))
        last[b] = n
    return out


class Count:

    def __init__(self, sem, per, before=0):
        self.sem, self.per, self.before = sem, per, before

    def at(self, i, n):
        return 1 + n if i is None else i * self.per + (1 + self.before + n)


def build(nc, x, w1, b1, w2, b2, hw_qkv, hb_qkv, hw_o, hb_o, ew_qkv, eb_qkv, ew_o, eb_o, out):
    ctx = ExitStack()
    with ctx:
        ctx.enter_context(nc.allow_non_contiguous_dma(reason="biases, once"))

        def sb(name, shape, dt=F32):
            return ctx.enter_context(nc.sbuf_tensor(name, shape, dt))

        def pb(name, shape):
            return ctx.enter_context(nc.psum_tensor(name, shape, F32))

        x_v = x.rearrange("b (k p) h w -> b k p (h w)", p=P)
        out_v = out.rearrange("b (k p) h w -> b k p (h w)", p=P)
        w_split = nc.dram_tensor("w_split", (16, P, 2048), F32, kind="Internal").ap()
        y_dram = nc.dram_tensor("y", (8, P, HALF), F32, kind="Internal").ap()

        w_qk = sb("w_qk", [P, 2, KC, 2, P], F32R)
        w_vo = sb("w_vo", [P, 2, 2, 2, C], F32R)
        xs = sb("xs", [P, 2, KC, N], F32R)
        qs = sb("qs", [P, 2, 2, N], F32R)
        qm = sb("qm", [P, 2, 2, N], F32R)
        kk = sb("kk", [P, 2, 2, N], F32R)
        kl = sb("kl", [P, 2, 2, N], F32R)
        v_y = sb("v_y", [P, NT, C])
        probs = sb("probs", [P, SLOTS_P, 2 * HALF])
        sums = [sb(f"sums{h}", [P, 2 * HALF]) for h in range(2)]
        o_t = sb("o_t", [P, 2, PAIRS, N], F32R)
        xin = sb("xin", [P, XIN, HALF])
        tmp = sb("tmp", [P, HALF])
        squares = sb("squares", [P, HALF])
        mxw = sb("mxw", [P, NT, 66], F32R)
        mxp = sb("mxp", [P, 2, NT, 2])
        ident = sb("ident", [P, P], F32R)
        group_mean = sb("group_mean", [P, P])
        ones = sb("ones", [P, HD])
        stats = sb("stats", [P, KC, 2, 6])
        mv = sb("mv", [P, KC, 2])
        gm = sb("gm", [P, KC])
        small = sb("small", [P, 8, KC])
        keep = sb("keep", [P, 2, KC])
        shift = sb("shift", [P, 2, KC])
        ss = sb("ss", [P, P])
        sc = sb("sc", [P, 4, P])
        y_scale = sb("y_scale", [P, P])
        bias_q = sb("bias_q", [P, 2, 3, KC])
        bias_o = sb("bias_o", [P, 2, KC])
        bias_1 = sb("bias_1", [P, 1])
        bias_2 = sb("bias_2", [P, KC])

        score_ps = [pb(f"score_ps{i}", [P, HALF]) for i in range(SCORE_BANKS)]
        acc_ps = [pb(f"acc_ps{i}", [P, HALF]) for i in range(2)]
        aux_ps = [pb(f"aux_ps{i}", [P, HALF]) for i in range(AUX_BANKS)]

        FIRST, AUX = aux_tiles(-1), aux_tiles(0) + aux_tiles(1)
        placed = {id(tiles): banks(tiles) for tiles in (FIRST, AUX)}

        def frees(tiles, e, n=None):
            return sum(last == e for _, last, _ in tiles[:n])

        at = {name: (tiles, n) for tiles in (FIRST, AUX) for n, (name, _, _) in enumerate(tiles)}

        def sem(name):
            return ctx.enter_context(nc.semaphore(name))

        def counted(name, per, before=0):
            return Count(sem(name), per, before)

        NSC = 4 * TILES
        NSUM = 2 * PAIRS * (NT - 1)
        s_const = sem("constants_set")
        s_ident = sem("identity_set")
        s_bias = sem("biases_loaded")
        s_raw = [sem(f"raw_weights_loaded{i}") for i in range(3)]
        s_split = sem("weights_split")
        s_wst = [sem(f"split_weights_stored{i}") for i in range(2)]
        c_wqk = counted("w_qk_loaded", 16 * 8, 32)
        c_wv = counted("w_v_loaded", 16 * 16)
        c_wo = counted("w_o_loaded", 16 * 4)
        c_xin = [counted(f"xin_loaded{q}", 16 * 42 // XIN, 16 * len([n for n in range(1, 27) if n % XIN == q]))
                 for q in range(XIN)]
        c_xfree = counted("xin_read", 40, 24)
        c_xm = counted("x_masked", 16, 8)
        c_xg = counted("x_scaled", 8, 8)
        c_keep = counted("masks_made", 1, 1)
        c_xa = counted("x_squared_or_hi", 24, 16)
        c_pe_in = counted("gate_operand_made", 4, 4)
        c_d2a = counted("operand_of_scale_made", 3, 3)
        c_a2d = counted("function_of_scale_made", 3, 3)
        c_yd2a = counted("operand_of_y_scale_made", 2)
        c_ya2d = counted("function_of_y_scale_made", 2)
        c_aux = counted("aux_made", len(AUX), len(FIRST))
        c_free = {e: counted(n, frees(AUX, e), frees(FIRST, e))
                  for e, n in (("A", "aux_read_by_scalar"), ("D", "aux_read_by_vector"),
                               ("Q", "qk_halved"), ("N", "sum_inverted"))}
        c_hi = counted("qk_hi_made", 128, 16)
        c_mx = counted("max_made", 16, 2)
        c_score = counted("scores_made", NSC)
        c_exp = counted("probs_made", NSC)
        c_pv = counted("probs_multiplied", 2 * TILES)
        c_sum = [counted(f"probs_summed{h}", NSUM) for h in range(2)]
        c_ln = counted("recip_guessed", 16)
        c_on = counted("o_normal", 16)
        c_ohi = counted("o_hi_made", 16)
        c_olo = counted("o_lo_made", 16)
        c_sq = counted("y_squared", 8)
        c_sqf = counted("y_square_read", 8)
        c_x = [counted(f"residual_loaded{k}", 16) for k in range(8)]
        c_vst = [counted(f"result_stored{k}", 32) for k in range(8)]
        c_dstep = counted("vector_step", DVE_STEPS, DVE_FIRST)
        c_astep = counted("scalar_step", ACT_STEPS, ACT_FIRST)
        COUNTS = [c_wqk, c_wv, c_wo, *c_xin, c_xfree, c_xm, c_xg, c_keep, c_xa, c_pe_in, c_d2a, c_a2d, c_yd2a, c_ya2d, c_aux,
                  *c_free.values(), c_hi, c_mx, c_score, c_exp, c_pv, *c_sum, c_ln, c_on, c_ohi, c_olo, c_sq,
                  c_sqf, *c_x, *c_vst, c_dstep, c_astep]

        def bank(name):
            tiles, n = at[name]
            return aux_ps[placed[id(tiles)][n][0]]

        def aux_made(eng, i, name):
            eng.wait_ge(c_aux.sem, c_aux.at(i, at[name][1] + 1))
            return bank(name)

        def aux_read(eng, i, name):
            tiles, n = at[name]
            e = tiles[n][1]
            eng.wait_ge(c_free[e].sem, c_free[e].at(i, frees(tiles, e, n + 1)))

        def bank_free(pe, i, name):
            tiles, n = at[name]
            last = placed[id(tiles)][n][1]
            if last is not None:
                aux_read(pe, i, tiles[last][0])
            elif tiles is AUX:
                for e in c_free.values():
                    pe.wait_ge(e.sem, e.at(i, 0))
            return bank(name)

        SRCS = []
        for wq, wo in ((hw_qkv, hw_o), (ew_qkv, ew_o)):
            r, ro = (a.rearrange("(k p) n -> p k n", p=P) for a in (wq, wo))
            for p in range(PAIRS):
                SRCS.append([(r[:, :, j * C + p * P:j * C + (p + 1) * P], j) for j in range(2)])
            SRCS += [[(r[:, 2 * c:2 * c + 2, 2 * C:3 * C], None)] for c in range(2)]
            SRCS += [[(ro[:, 2 * c:2 * c + 2, :], None)] for c in range(2)]
        raw_at, count = [], [0] * 3
        for c, parts in enumerate(SRCS):
            count[c % 3] += 16 * len(parts)
            raw_at.append(count[c % 3])

        def token_half(h):
            return slice(h * HALF, (h + 1) * HALF)

        def xin_slot(t, kind, j):
            return xin[:, chunk_at(t, kind, j)[0] % XIN, :]

        def chunk_in(eng, i, t, kind, j):
            n = chunk_at(t, kind, j)[0]
            q = n % XIN
            loads = (n - q) // XIN + 1 - (t < 0 and q == 0)
            eng.wait_ge(c_xin[q].sem, c_xin[q].at(i, 16 * loads))
            return xin_slot(t, kind, j)

        def x_chunk(j):
            return j // 2, token_half(j % 2)

        def new_image(t):
            return t != 0

        def before_stats(t):
            return 8 if t == 1 else 0

        def chunk_at(t, kind, j):
            if t == 0:
                return j, j
            b = 8 if t == 1 else 1
            load = b + {"stats": 0, "w": 8, "norm": 10, "operand": 18, "y": 26}[kind] + j
            return load, load - (b - before_stats(t)) - (0 if kind in ("stats", "w") else 2)

        def from_scalar_at(t, kind, j):
            return j if t == 0 else before_stats(t) + (8 if kind == "operand" else 0) + j

        def masked_at(t, j):
            return before_stats(t) + j

        def owner(t, p):
            return (t, p) if p < PAIRS else ((t + 1) % 2, 0)

        def nth_pair(t, p):
            return 0 if t < 0 else PAIRS * t + p - 1

        block = ctx.enter_context(nc.Block())

        @block.sync
        def _(sp):
            for c in COUNTS:
                sp.sem_inc(c.sem, 1)
            for t, (bq, bo) in enumerate(((hb_qkv, hb_o), (eb_qkv, eb_o))):
                for j in range(3):
                    sp.dma_start(bias_q[:, t, j, :], bq[j * C:(j + 1) * C].rearrange("(k p) -> p k", p=P)).then_inc(s_bias, 16)
                sp.dma_start(bias_o[:, t, :], bo.rearrange("(k p) -> p k", p=P)).then_inc(s_bias, 16)
            sp.dma_start(bias_1[:, :], b1.rearrange("(p a) -> p a", a=1)).then_inc(s_bias, 16)
            sp.dma_start(bias_2[:, :], b2.rearrange("(k p) -> p k", p=P)).then_inc(s_bias, 16)

            def store_split(c):
                sp.wait_ge(s_split, 2 * c + 2)
                sp.dma_start(w_split[c], o_t[:, c % 2, 0:2, :].rearrange("p a n -> p (a n)").bitcast(F32)).then_inc(s_wst[c % 2], 16)

            for c, parts in enumerate(SRCS):
                if c >= 3:
                    sp.wait_ge(s_split, 2 * (c - 2))
                raw = probs[:, c % 3, :]
                for src, j in parts:
                    dst = (raw.rearrange("p (k n) -> p k n", k=2) if j is None
                           else raw.rearrange("p (k j n) -> p k j n", k=KC, j=2)[:, :, j, :])
                    sp.dma_start(dst, src).then_inc(s_raw[c % 3], 16)
                if c >= 2:
                    store_split(c - 2)
            store_split(14)
            store_split(15)

            def load_x(i, t, kind, j, src):
                n = chunk_at(t, kind, j)[0]
                last = [(kd, jj) for kd, count in (("stats", 8), ("w", 2), ("norm", 8), ("operand", 8), ("y", 8))
                        for jj in range(count) if t and chunk_at(t, kd, jj)[0] == n - XIN]
                if last and last[0][0] == "w":
                    sp.wait_ge(c_aux.sem, c_aux.at(i, at[(t, ("hidden", "gate")[last[0][1]])][1] + 1))
                elif last:
                    sp.wait_ge(c_xfree.sem, c_xfree.at(i, chunk_at(t, *last[0])[1] + 1))
                elif i is not None:
                    sp.wait_ge(c_xfree.sem, c_xfree.at(i, max(n - XIN + 1, 0)))
                dst = xin[:, n % XIN, :]
                sp.dma_start(dst.rearrange("p (k n) -> p k n", k=KC) if (kind, j) == ("w", 0) else dst,
                             src).then_inc(c_xin[n % XIN].sem, 16)

            def load_chunks(i, t, kind, chunks, next_image=None):
                image = 0 if i is None else i if t == 0 else next_image
                for j in chunks:
                    k, cols = x_chunk(j)
                    load_x(i, t, kind, j, x_v[image, k, :, cols])

            def load_gate(i, t):
                load_x(i, t, "w", 0, w1.rearrange("(k p) n -> p k n", p=P))
                load_x(i, t, "w", 1, w2)

            def load_qk(t, p):
                t, p = owner(t, p)
                sp.dma_start(w_qk[:, :, :, :, :].rearrange("p a k j n -> p (a k j n)").bitcast(F32),
                             w_split[8 * t + p]).then_inc(c_wqk.sem, 16)

            load_chunks(None, -1, "stats", range(8))
            load_gate(None, -1)
            load_chunks(None, -1, "norm", range(8))
            load_chunks(None, -1, "operand", range(8))
            for q in s_wst:
                sp.wait_ge(q, 16 * 8)
            load_qk(-1, PAIRS)
            sp.wait_ge(c_aux.sem, c_aux.at(None, at[(-1, "qk", PAIRS, 3)][1] + 1))
            load_qk(0, 1)
            with sp.Fori(0, B) as i:
                next_image = sp.snap(sp.to_reg((i + 1) & (B - 1)))
                for t in range(2):
                    for ct in range(4):
                        if t:
                            sp.wait_ge(c_aux.sem, c_aux.at(i, at[(0, "o", 4 + ct)][1] + 1))
                        else:
                            sp.wait_ge(c_aux.sem, c_aux.at(i, ct - 3))
                        for c in range(2):
                            sp.dma_start(w_vo[:, c, :, :, ct * P:(ct + 1) * P].rearrange("p a k n -> p (a k) n").bitcast(F32),
                                         w_split[8 * t + 4 + c].rearrange("p (a n) -> p a n", a=4)[:, :, ct * P:(ct + 1) * P]
                                         ).then_inc(c_wv.sem, 16)

                    def next_qk(t, p, made, k):
                        sp.wait_ge(c_aux.sem, c_aux.at(i, at[(t, "qk", made, k)][1] + 1))
                        load_qk(*owner(t, p))

                    next_qk(t, 2, 1, 3)
                    sp.wait_ge(c_aux.sem, c_aux.at(i, at[(t, "v", NT - 1)][1] + 1))
                    for c in range(2):
                        sp.dma_start(w_vo[:, c, :, :, :].rearrange("p a k n -> p (a k n)").bitcast(F32),
                                     w_split[8 * t + 6 + c]).then_inc(c_wo.sem, 16)

                    if new_image(t):
                        load_chunks(i, t, "stats", range(8), next_image)
                        load_gate(i, t)
                    next_qk(t, 3, 2, 3)
                    if new_image(t):
                        load_chunks(i, t, "norm", range(8), next_image)
                    load_chunks(i, t, "operand", range(2), next_image)
                    next_qk(t, 4, 3, 3)
                    load_chunks(i, t, "operand", range(2, 8), next_image)
                    sp.wait_ge(c_aux.sem, c_aux.at(i, at[(t, "qk", PAIRS, 3)][1] + 1))
                    load_qk(1 - t, 1)

                    def tile_of(dram, k):
                        return dram[i, k % 4, :, token_half(k // 4)]

                    for k in range(8):
                        if t:
                            sp.wait_ge(c_pv.sem, c_pv.at(i, 2 * TILES - NT + k + 1))
                            sp.dma_start(v_y[:, k, :], tile_of(x_v, k)).then_inc(c_x[k].sem, 16)
                            load_x(i, t, "y", k, y_dram[k])
                    for k in range(8):
                        aux_read(sp, i, (t, "o", k))
                        sp.dma_start(tile_of(out_v, k) if t else y_dram[k], v_y[:, k, :]).then_inc(c_vst[k].sem, 16)
            for c in c_vst:
                sp.wait_ge(c.sem, 1 + B * 32)
            sp.wait_ge(c_wqk.sem, 33 + B * 128)

        @block.gpsimd
        def _(pool):
            pool.memset(tmp[:, 0:P], 0.0).then_inc(s_const, 1)
            pool.memset(group_mean[:, :], 1.0 / GROUP).then_inc(s_const, 1)
            pool.memset(ones[:, :], 1.0).then_inc(s_const, 1)
            pool.memset(mxw[:, :, :].bitcast(F32), 0.0).then_inc(s_const, 1)
            pool.memset(qm[:, :, :, :].bitcast(F32), 0.0).then_inc(s_const, 1)
            pool.memset(kl[:, :, :, :].bitcast(F32), 1.0).then_inc(s_const, 1)
            pool.wait_ge(s_const, 6)
            pool.affine_select(out=tmp[:, 0:P], in_=tmp[:, 0:P], compare_op=ALU.not_equal,
                               fill=1.0, base=0, pattern=[[-1, P]], channel_multiplier=1).then_inc(s_const, 1)
            g3 = group_mean[:, :].rearrange("p (g c) -> p g c", c=GROUP)
            pool.affine_select(out=g3, in_=g3, compare_op=ALU.is_ge, fill=0.0, base=0,
                               pattern=[[-GROUP, P // GROUP], [0, GROUP]], channel_multiplier=1).then_inc(s_const, 1)
            pool.wait_ge(s_const, 8)
            pool.affine_select(out=g3, in_=g3, compare_op=ALU.is_ge, fill=0.0, base=GROUP - 1,
                               pattern=[[GROUP, P // GROUP], [0, GROUP]], channel_multiplier=-1).then_inc(s_const, 1)
            with pool.Fori(0, B) as i:
                for t in range(2):
                    for ph in range(2 * PAIRS):
                        p, h = ph // 2, ph % 2
                        for m in range(1, NT):
                            g = TILES * t + 8 * ph + m
                            n = NSUM // 2 * t + (NT - 1) * p + m - 1
                            pool.wait_ge(c_exp.sem, c_exp.at(i, 2 * g + 2))
                            if m == 1 and p:
                                pool.wait_ge(c_aux.sem, c_aux.at(i, at[(t, "den", ph - 2)][1] + 1))
                            pool.wait_ge(c_sum[h].sem, c_sum[h].at(i, n))
                            a = probs[:, (g - 1) % SLOTS_P, :] if m == 1 else sums[h][:, :]
                            pool.tensor_tensor(sums[h][:, :], a, probs[:, g % SLOTS_P, :], ALU.add).then_inc(c_sum[h].sem, 1)

        @block.scalar
        def _(act):
            act.preload_act_table_set("natural_log_exp_and_others")
            act.wait_ge(s_bias, 16 * 10)
            act.wait_ge(s_ident, 1)
            steps = [0]

            def step(i, ins):
                steps[0] += 1
                ins.then_inc(c_astep.sem, 1)
                act.wait_ge(c_astep.sem, c_astep.at(i, steps[0]))

            def power(i, dst, src, e, made):
                step(i, act.activation(dst, src, ACT.Ln))
                act.activation(dst, dst, ACT.Exp, scale=e).then_inc(made.sem, 1)

            def operand_step(i, t, g):
                if new_image(t):
                    if g == RSTD_IN:
                        act.wait_ge(c_d2a.sem, c_d2a.at(i, 1))
                        power(i, small[:, 3, :], small[:, 2, :], -0.5, c_a2d)
                    if NORMS <= g < NORMS + 8:
                        j = g - NORMS
                        k = j // 2
                        if j == 0:
                            act.wait_ge(c_keep.sem, c_keep.at(i, 1))
                        chunk = chunk_in(act, i, t, "norm", j)
                        if j:
                            act.wait_ge(c_xfree.sem, c_xfree.at(i, chunk_at(t, "norm", j)[1]))
                        elif i is not None:
                            act.wait_ge(c_sqf.sem, c_sqf.at(i, 8))
                        act.activation(squares[:, :], chunk, ACT.Square, bias=shift[:, 0, k:k + 1],
                                       scale=keep[:, 0, k:k + 1]).then_inc(c_xa.sem, 1)
                    if g == RNORM:
                        act.wait_ge(c_d2a.sem, c_d2a.at(i, 2))
                        power(i, sc[:, 0, :], ss[:, :], -0.5, c_a2d)
                    if g == EXP2N:
                        act.wait_ge(c_d2a.sem, c_d2a.at(i, 3))
                        act.activation(sc[:, 2, :], sc[:, 1, :], ACT.Exp, scale=2.0).then_inc(c_a2d.sem, 1)
                if OPERAND <= g < OPERAND + 8:
                    j = g - OPERAND
                    k, cols = x_chunk(j)
                    if new_image(t):
                        act.wait_ge(c_xg.sem, c_xg.at(i, j + 1))
                    else:
                        act.wait_ge(c_xm.sem, c_xm.at(i, masked_at(t, j) + 1))
                    if j == 0 and i is not None:
                        act.wait_ge(c_aux.sem, c_aux.at(i, at[(t, "qk", PAIRS - 1, 3)][1] + 1))
                    act.activation(xs[:, 0, k, cols], xin_slot(t, "operand", j), ACT.Copy).then_inc(c_xa.sem, 1)
                if OPERAND <= g + 1 < OPERAND + 8:
                    j = g + 1 - OPERAND
                    k, a = j // 2, 0 if new_image(t) else 1
                    chunk = chunk_in(act, i, t, "operand", j)
                    act.activation(chunk, chunk, ACT.Identity, bias=shift[:, a, k:k + 1],
                                   scale=keep[:, a, k:k + 1]).then_inc(c_xm.sem, 1)

            def qk_hi(i, t, p, k):
                what, h = QK[k]
                ps = aux_made(act, i, (t, "qk", p, k))
                cols = token_half(h)
                tt, pp = owner(t, p)
                for j, (lo, hi) in enumerate(((0, HD), (HD, P))):
                    b = bias_q[lo:hi, tt, what, pp:pp + 1]
                    dsts = ((qs[lo:hi, p % 2, j, cols], qm[lo:hi, p % 2, j, cols]) if what == 0 else
                            (kk[0:HD, p % 2, j, cols], kk[HD:P, p % 2, j, cols]))
                    for d in dsts:
                        act.activation(d, ps[lo:hi, :], ACT.Identity, bias=b).then_inc(c_hi.sem, 1)

            def neg_rows(i, t, p):
                for h in range(2):
                    ps = aux_made(act, i, (t, "neg", p, h))
                    cols = token_half(h)
                    step(i, act.activation(qm[HD:HD + 1, p % 2, 0, cols], ps[HD:HD + 1, :], ACT.Copy))
                    act.activation(qm[0:1, p % 2, 1, cols], ps[0:1, :], ACT.Copy).then_inc(c_free["A"].sem, 1)

            for g in range(STEPS_END):
                operand_step(None, -1, g)
            for k in range(4):
                qk_hi(None, -1, PAIRS, k)
            neg_rows(None, -1, PAIRS)
            assert steps[0] == ACT_FIRST, ("ACT_FIRST", steps[0])
            steps[0] = 0
            with act.Fori(0, B) as i:
                for t in range(2):

                    def exps(g):
                        n = TILES * t + g
                        last = max(n - SLOTS_P, -1)
                        act.wait_ge(c_pv.sem, c_pv.at(i, last + 1))
                        if last >= 0:
                            act.wait_ge(c_sum[(last // 8) % 2].sem,
                                        c_sum[(last // 8) % 2].at(i, (NT - 1) * (last // 16) + max(last % 8, 1)))
                        else:
                            act.wait_ge(c_sum[1].sem, c_sum[1].at(i, 0))
                        for u in (2 * n, 2 * n + 1):
                            act.wait_ge(c_score.sem, c_score.at(i, u + 1))
                            act.activation(probs[:, n % SLOTS_P, token_half(u % 2)], score_ps[u % SCORE_BANKS][:, :],
                                           ACT.Exp, scale=SCALE).then_inc(c_exp.sem, 1)

                    def recip_guess(ph):
                        ps = aux_made(act, i, (t, "den", ph))
                        act.wait_ge(c_on.sem, c_on.at(i, 8 * t + ph))
                        power(i, tmp[:, :], ps[:, :], -1.0, c_ln)

                    def o_hi(ph):
                        p, h = ph // 2, ph % 2
                        act.wait_ge(c_on.sem, c_on.at(i, 8 * t + ph + 1))
                        act.activation(o_t[:, 0, p, token_half(h)], acc_ps[ph % 2][:, :],
                                       ACT.Identity, bias=bias_q[:, t, 2, p:p + 1]).then_inc(c_ohi.sem, 1)

                    def v_out(m):
                        ps = aux_made(act, i, (t, "v", m))
                        act.wait_ge(c_vst[m].sem, c_vst[m].at(i, 16 * t))
                        act.activation(v_y[:, m, :], ps[:, :], ACT.Copy).then_inc(c_free["A"].sem, 1)

                    exps(0)
                    for k in range(4):
                        qk_hi(i, t, 1, k)
                    v_out(0)
                    for g in range(TILES):
                        p, r = g // 16, g % 16
                        if g + 1 < TILES:
                            exps(g + 1)
                        if r == NEG:
                            neg_rows(i, t, p + 1)
                        for f in projection(g):
                            if f[0] == "qk":
                                qk_hi(i, t, f[1], f[2])
                            else:
                                v_out(f[1])
                        if g in DENS:
                            recip_guess(DENS[g])
                        if g - 2 in DENS:
                            o_hi(DENS[g - 2])
                        if t and g - 1 == Y_RNORM:
                            act.wait_ge(c_yd2a.sem, c_yd2a.at(i, 1))
                            power(i, sc[:, 0, :], ss[:, :], -0.5, c_ya2d)
                        if t and g - 1 == Y_LOGS:
                            act.wait_ge(c_yd2a.sem, c_yd2a.at(i, 2))
                            step(i, act.activation(sc[:, 2, :], sc[:, 1, :], ACT.Ln, bias=1.0))
                            act.activation(sc[:, 3, :], sc[:, 1, :], ACT.Ln, bias=1.0, scale=-1.0).then_inc(c_ya2d.sem, 1)
                        if g:
                            operand_step(i, t, g - 1)

                    def y_out(k):
                        ps = aux_made(act, i, (0, "o", k))
                        act.activation(v_y[:, k, :], ps[:, :], ACT.Identity,
                                       bias=bias_o[:, 0, k % 4:k % 4 + 1]).then_inc(c_free["A"].sem, 1)
                        aux_read(act, i, (0, "o", k))
                        if k:
                            act.wait_ge(c_sqf.sem, c_sqf.at(i, k))
                        else:
                            act.wait_ge(c_xfree.sem, c_xfree.at(i, 0))
                        act.activation(squares[:, :], v_y[:, k, :], ACT.Square).then_inc(c_sq.sem, 1)

                    recip_guess(2 * PAIRS - 1)
                    if t == 0:
                        y_out(0)
                    o_hi(2 * PAIRS - 1)
                    if t == 0:
                        for k in range(1, 8):
                            y_out(k)
                assert steps[0] == ACT_STEPS, ("ACT_STEPS", steps[0])

        @block.vector
        def _(dve):
            for c in range(len(SRCS)):
                dve.wait_ge(s_raw[c % 3], raw_at[c])
                if c >= 2:
                    dve.wait_ge(s_wst[c % 2], 16 * (c // 2))
                dve.tensor_copy(o_t[:, c % 2, 0, :], probs[:, c % 3, :]).then_inc(s_split, 1)
                dve.wait_ge(s_split, 2 * c + 1)
                dve.tensor_tensor(o_t[:, c % 2, 1, :], probs[:, c % 3, :], o_t[:, c % 2, 0, :].bitcast(F32),
                                  ALU.subtract).then_inc(s_split, 1)
            dve.wait_ge(s_const, 9)
            dve.tensor_copy(ident[:, :], tmp[:, 0:P]).then_inc(s_ident, 1)
            dve.wait_ge(s_ident, 1)
            dve.wait_ge(s_bias, 16 * 10)
            steps = [0]

            def step(i, ins):
                steps[0] += 1
                ins.then_inc(c_dstep.sem, 1)
                dve.wait_ge(c_dstep.sem, c_dstep.at(i, steps[0]))

            def newton_rsqrt(i, r, v, work):
                step(i, dve.tensor_tensor(work, r, r, ALU.mult))
                step(i, dve.tensor_tensor(work, work, v, ALU.mult))
                step(i, dve.scalar_tensor_tensor(work, work, 3.0, r, ALU.subtract, ALU.mult))
                step(i, dve.tensor_scalar(r, work, -0.5, None, ALU.mult))

            def series(i, dst, s, coefs):
                step(i, dve.tensor_scalar(dst, s, coefs[-1], None, ALU.mult))
                for c in coefs[-2:0:-1]:
                    step(i, dve.scalar_tensor_tensor(dst, dst, c, s, ALU.add, ALU.mult))
                step(i, dve.tensor_scalar(dst, dst, coefs[0], None, ALU.add))

            def blend(i, dst, small_one, s, below):
                step(i, dve.tensor_scalar(s, s, below, None, ALU.is_lt))
                step(i, dve.tensor_tensor(small_one, small_one, dst, ALU.subtract))
                step(i, dve.tensor_tensor(small_one, small_one, s, ALU.mult))
                step(i, dve.tensor_tensor(dst, dst, small_one, ALU.add))

            def rows(ap):
                return ap.rearrange("p (r w) -> p r w", w=W)

            def per_row(a, k0):
                return sc[:, a, k0:k0 + ROWS].unsqueeze(2).to_broadcast([P, ROWS, W])

            def operand_step(i, t, g):
                if new_image(t):
                    if STATS <= g < STATS + 8:
                        j = g - STATS
                        dve.bn_stats(stats[:, j // 2, j % 2, :], chunk_in(dve, i, t, "stats", j)).then_inc(c_xfree.sem, 1)
                    if g == AGGREGATE:
                        dve.wait_ge(c_xfree.sem, c_xfree.at(i, chunk_at(t, "stats", 7)[1] + 1))
                        dve.memset(small[:, 7, :], 0.0)
                        for k in range(KC):
                            last = dve.bn_aggr(mv[:, k, :], stats[:, k, :, :].rearrange("p h s -> p (h s)"))
                        last.then_inc(c_pe_in.sem, 1)
                    if g == MEAN:
                        ps = aux_made(dve, i, (t, "mean"))
                        dve.tensor_copy(gm[:, :], ps[:, 0:KC]).then_inc(c_free["D"].sem, 1)
                        aux_read(dve, i, (t, "mean"))
                        step(i, dve.tensor_tensor(small[:, 1, :], mv[:, :, 0], gm[:, :], ALU.subtract))
                        step(i, dve.tensor_tensor(small[:, 0, :], small[:, 1, :], small[:, 1, :], ALU.mult))
                        dve.tensor_tensor(small[:, 0, :], small[:, 0, :], mv[:, :, 1], ALU.add).then_inc(c_pe_in.sem, 1)
                    if g == VAR:
                        ps = aux_made(dve, i, (t, "var"))
                        dve.tensor_scalar(small[:, 2, :], ps[:, 0:KC], GN_EPS, None, ALU.add).then_inc(c_free["D"].sem, 1)
                        aux_read(dve, i, (t, "var"))
                        dve.tensor_copy(small[:, 6, :], small[:, 2, :]).then_inc(c_d2a.sem, 1)
                    if g == RSTD:
                        dve.wait_ge(c_a2d.sem, c_a2d.at(i, 1))
                        newton_rsqrt(i, small[:, 3, :], small[:, 2, :], small[:, 4, :])
                        dve.tensor_tensor(small[:, 0, :], small[:, 1, :], small[:, 3, :], ALU.mult).then_inc(c_pe_in.sem, 1)
                    if g == HIDDEN_AT:
                        ps = aux_made(dve, i, (t, "hidden"))
                        dve.tensor_scalar(small[:, 4, 0:1], ps[:, 0:1], bias_1[:, 0:1], None, ALU.add).then_inc(c_free["D"].sem, 1)
                        aux_read(dve, i, (t, "hidden"))
                        dve.tensor_scalar(small[:, 5, 0:1], small[:, 4, 0:1], 0.0, None, ALU.max).then_inc(c_pe_in.sem, 1)
                    if g == GATE_AT:
                        ps = aux_made(dve, i, (t, "gate"))
                        dve.tensor_tensor(small[:, 4, :], ps[:, 0:KC], bias_2[:, :], ALU.add).then_inc(c_free["D"].sem, 1)
                        aux_read(dve, i, (t, "gate"))
                        step(i, dve.tensor_scalar(small[:, 5, :], small[:, 4, :], 0.0, None, ALU.is_gt))
                        step(i, dve.tensor_tensor(keep[:, 0, :], small[:, 3, :], small[:, 5, :], ALU.mult))
                        step(i, dve.tensor_tensor(keep[:, 1, :], small[:, 3, :], keep[:, 0, :], ALU.subtract))
                        for a in range(2):
                            last = dve.scalar_tensor_tensor(shift[:, a, :], gm[:, :], -1.0, keep[:, a, :], ALU.mult, ALU.mult)
                        last.then_inc(c_keep.sem, 1)
                    if NORMS < g <= NORMS + 8:
                        j = g - NORMS - 1
                        dve.wait_ge(c_xa.sem, c_xa.at(i, from_scalar_at(t, "norm", j) + 1))
                        dve.tensor_reduce(ss[:, j * ROWS:(j + 1) * ROWS], rows(squares[:, :]), AX.X,
                                          ALU.add).then_inc(c_xfree.sem, 1)
                    if g == CLAMP:
                        dve.wait_ge(c_xfree.sem, c_xfree.at(i, chunk_at(t, "norm", 7)[1] + 1))
                        dve.tensor_scalar(ss[:, :], ss[:, :], 2.0 ** -60, None, ALU.max).then_inc(c_d2a.sem, 1)
                    if g == NORM:
                        dve.wait_ge(c_a2d.sem, c_a2d.at(i, 2))
                        newton_rsqrt(i, sc[:, 0, :], ss[:, :], sc[:, 1, :])
                        step(i, dve.tensor_tensor(sc[:, 1, :], ss[:, :], sc[:, 0, :], ALU.mult))
                        dve.tensor_scalar(sc[:, 1, :], sc[:, 1, :], 20.0, None, ALU.min).then_inc(c_d2a.sem, 1)
                    if g == EXP2N:
                        step(i, dve.tensor_scalar(ss[:, :], ss[:, :], 1.0, None, ALU.min))
                        series(i, sc[:, 3, :], ss[:, :], TANH_SERIES)
                    if g == SCALES:
                        dve.wait_ge(c_a2d.sem, c_a2d.at(i, 3))
                        step(i, dve.tensor_scalar(sc[:, 2, :], sc[:, 2, :], 1.0, None, ALU.add))
                        step(i, dve.reciprocal(sc[:, 1, :], sc[:, 2, :]))
                        step(i, dve.tensor_scalar(sc[:, 1, :], sc[:, 1, :], -2.0, 1.0, ALU.mult, ALU.add))
                        step(i, dve.tensor_tensor(sc[:, 1, :], sc[:, 1, :], sc[:, 0, :], ALU.mult))
                        blend(i, sc[:, 1, :], sc[:, 3, :], ss[:, :], TANH_BELOW)
                if OPERAND < g <= OPERAND + 8:
                    j = g - OPERAND - 1
                    k, cols = x_chunk(j)
                    dve.wait_ge(c_xa.sem, c_xa.at(i, from_scalar_at(t, "operand", j) + 1))
                    dve.tensor_tensor(xs[:, 1, k, cols], xin_slot(t, "operand", j), xs[:, 0, k, cols].bitcast(F32),
                                      ALU.subtract).then_inc(c_xfree.sem, 1)
                if new_image(t) and OPERAND <= g < OPERAND + 8:
                    j = g - OPERAND
                    dve.wait_ge(c_xm.sem, c_xm.at(i, masked_at(t, j) + 1))
                    chunk = rows(xin_slot(t, "operand", j))
                    dve.tensor_tensor(chunk, chunk, per_row(1, j * ROWS), ALU.mult).then_inc(c_xg.sem, 1)

            def y_scale_step(i, g):
                if g == Y_RNORM:
                    dve.wait_ge(c_sqf.sem, c_sqf.at(i, 8))
                    dve.tensor_scalar(ss[:, :], ss[:, :], 2.0 ** -60, None, ALU.max).then_inc(c_yd2a.sem, 1)
                if g == Y_NORM:
                    dve.wait_ge(c_ya2d.sem, c_ya2d.at(i, 1))
                    newton_rsqrt(i, sc[:, 0, :], ss[:, :], sc[:, 1, :])
                    step(i, dve.tensor_tensor(sc[:, 1, :], ss[:, :], sc[:, 0, :], ALU.mult))
                    dve.tensor_scalar(sc[:, 1, :], sc[:, 1, :], float(np.float32(1.0) - np.float32(EPS)), None,
                                      ALU.min).then_inc(c_yd2a.sem, 1)
                if g == Y_SCALE:
                    dve.wait_ge(c_ya2d.sem, c_ya2d.at(i, 2))
                    step(i, dve.tensor_tensor(sc[:, 3, :], sc[:, 2, :], sc[:, 3, :], ALU.subtract))
                    step(i, dve.scalar_tensor_tensor(y_scale[:, :], sc[:, 3, :], 0.5, sc[:, 0, :], ALU.mult, ALU.mult))
                    step(i, dve.tensor_scalar(ss[:, :], ss[:, :], 1.0, None, ALU.min))
                    series(i, sc[:, 1, :], ss[:, :], ATANH_SERIES)
                    blend(i, y_scale[:, :], sc[:, 1, :], ss[:, :], ATANH_BELOW)

            def y_sum(i, k):
                chunk = chunk_in(dve, i, 1, "y", k)
                scales = y_scale[:, k * ROWS:(k + 1) * ROWS].unsqueeze(2).to_broadcast([P, ROWS, W])
                step(i, dve.tensor_tensor(rows(chunk), rows(chunk), scales, ALU.mult))
                dve.wait_ge(c_x[k].sem, c_x[k].at(i, 16))
                dve.tensor_tensor(v_y[:, k, :], v_y[:, k, :], chunk, ALU.add).then_inc(c_xfree.sem, 1)

            def qk_lo(i, t, p, k):
                what, h = QK[k]
                ps = aux_made(dve, i, (t, "qk", p, k))
                dve.wait_ge(c_hi.sem, c_hi.at(i, 4 * (4 * nth_pair(t, p) + k + 1)))
                cols = token_half(h)
                tt, pp = owner(t, p)
                for j, (lo, hi) in enumerate(((0, HD), (HD, P))):
                    high = (qs, kk)[what][lo:hi, p % 2, j, cols].bitcast(F32)
                    dst = qs[P - hi:P - lo, p % 2, j, cols] if what == 0 else kl[lo:hi, p % 2, j, cols]
                    ins = dve.scalar_tensor_tensor(dst, ps[lo:hi, :], bias_q[lo:hi, tt, what, pp:pp + 1], high,
                                                   ALU.add, ALU.subtract)
                ins.then_inc(c_free["Q"].sem, 1)

            def max_tile(i, t, p, k):
                j, n, h = MAX_ORDER[k]
                ps = aux_made(dve, i, (t, "max", p, k))
                if k == 0 and i is not None:
                    dve.wait_ge(c_mx.sem, c_mx.at(i, 2 * nth_pair(t, p)))
                dve.tensor_reduce(mxp[:, j, n, h:h + 1], ps[:, :], AX.X, ALU.max).then_inc(c_free["D"].sem, 1)

            def combine(i, t, p):
                aux_read(dve, i, (t, "max", p, 31))
                for j in range(2):
                    dve.tensor_reduce(mxw[:, :, HD * (1 - j)], mxp[:, j, :, :], AX.X, ALU.max,
                                      negate=True).then_inc(c_mx.sem, 1)

            for g in range(STEPS_END):
                operand_step(None, -1, g)
            for k in range(4):
                qk_lo(None, -1, PAIRS, k)
            for k in range(32):
                max_tile(None, -1, PAIRS, k)
            combine(None, -1, PAIRS)
            assert steps[0] == DVE_FIRST, ("DVE_FIRST", steps[0])
            steps[0] = 0
            with dve.Fori(0, B) as i:
                for t in range(2):

                    def normalise(ph):
                        ps = aux_made(dve, i, (t, "den", ph))
                        dve.wait_ge(c_ln.sem, c_ln.at(i, 8 * t + ph + 1))
                        step(i, dve.tensor_tensor(ps[:, :], ps[:, :], tmp[:, :], ALU.mult))
                        dve.scalar_tensor_tensor(tmp[:, :], ps[:, :], 2.0, tmp[:, :], ALU.subtract,
                                                 ALU.mult).then_inc(c_free["N"].sem, 1)
                        aux_read(dve, i, (t, "den", ph))
                        acc = acc_ps[ph % 2]
                        dve.scalar_tensor_tensor(acc[:, :], acc[:, :], -1.0, tmp[:, :], ALU.mult,
                                                 ALU.mult).then_inc(c_on.sem, 1)

                    def o_lo(ph):
                        p, h = ph // 2, ph % 2
                        dve.wait_ge(c_ohi.sem, c_ohi.at(i, 8 * t + ph + 1))
                        dve.scalar_tensor_tensor(o_t[:, 1, p, token_half(h)], acc_ps[ph % 2][:, :],
                                                 bias_q[:, t, 2, p:p + 1], o_t[:, 0, p, token_half(h)].bitcast(F32),
                                                 ALU.add, ALU.subtract).then_inc(c_olo.sem, 1)

                    for k in range(4):
                        qk_lo(i, t, 1, k)
                    for g in range(TILES):
                        p, r = g // 16, g % 16
                        if r == COMBINE:
                            combine(i, t, p + 1)
                        if g - 3 in DENS:
                            o_lo(DENS[g - 3])
                        for f in maxes(g):
                            max_tile(i, t, f[1], f[2])
                        for f in projection(g - 1):
                            if f[0] == "qk":
                                qk_lo(i, t, f[1], f[2])
                        if g - 1 in DENS:
                            normalise(DENS[g - 1])
                        if t:
                            y_scale_step(i, g)
                        if t and Y_SUM <= g < TILES:
                            y_sum(i, g - Y_SUM)
                        operand_step(i, t, g)
                    normalise(2 * PAIRS - 1)
                    o_lo(2 * PAIRS - 1)
                    if t == 0:
                        for k in range(8):
                            dve.wait_ge(c_sq.sem, c_sq.at(i, k + 1))
                            dve.tensor_reduce(ss[:, k * ROWS:(k + 1) * ROWS], rows(squares[:, :]), AX.X,
                                              ALU.add).then_inc(c_sqf.sem, 1)
                    else:
                        for k in range(8):
                            if 2 <= k < 4:
                                y_sum(i, k + 4)
                            ps = aux_made(dve, i, (1, "o", k))
                            dve.scalar_tensor_tensor(v_y[:, k, :], ps[:, :], bias_o[:, 1, k % 4:k % 4 + 1], v_y[:, k, :],
                                                     ALU.add, ALU.add).then_inc(c_free["D"].sem, 1)
                assert steps[0] == DVE_STEPS, ("DVE_STEPS", steps[0])

        @block.tensor
        def _(pe):
            pe.wait_ge(s_const, 9)
            pe.wait_ge(s_ident, 1)

            def halves(ps, lhs, rhs):
                todo = [(k, a, b) for k in range(KC) for a, b in ((0, 0), (0, 1), (1, 0))]
                for n, (k, a, b) in enumerate(todo):
                    last = nc.tensor.matmul(ps, lhs(a, k), rhs(b, k), start=(n == 0), stop=(n == len(todo) - 1))
                return last

            def gate_tile(i, t, g):
                name = GATE_TILES[g]
                ps = bank_free(pe, i, (t, name))
                pe.wait_ge(c_pe_in.sem, c_pe_in.at(i, sorted(GATE_TILES).index(g) + 1))
                if name == "mean":
                    nc.tensor.matmul(ps[:, 0:KC], group_mean[:, :], mv[:, :, 0], start=True, stop=True).then_inc(c_aux.sem, 1)
                if name == "var":
                    nc.tensor.matmul(ps[:, 0:KC], group_mean[:, :], small[:, 0, :], start=True, stop=True).then_inc(c_aux.sem, 1)
                w = {"hidden": 0, "gate": 1}.get(name)
                if w is not None:
                    weights = chunk_in(pe, i, t, "w", w)
                    for k in range(KC):
                        if w == 0:
                            last = nc.tensor.matmul(ps[:, 0:1], weights[:, k * HIDDEN:(k + 1) * HIDDEN],
                                                    small[:, 0, k:k + 1], start=(k == 0), stop=(k == KC - 1))
                        else:
                            last = nc.tensor.matmul(ps[:, k:k + 1], weights[:, k * P:(k + 1) * P], small[:, 5, 0:1],
                                                    start=True, stop=True)
                    last.then_inc(c_aux.sem, 1)

            def qk_tile(i, t, p, k):
                what, h = QK[k]
                ps = bank_free(pe, i, (t, "qk", p, k))
                if k == 0:
                    pe.wait_ge(c_wqk.sem, c_wqk.at(i, 16 * (1 if t < 0 else 4 * t + p - 1)))
                    if p == PAIRS:
                        pe.wait_ge(c_xfree.sem, c_xfree.at(i, chunk_at(t, "operand", 7)[1] + 1))
                halves(ps[:, :], lambda a, c: w_qk[:, a, c, what, :],
                       lambda b, c: xs[:, b, c, token_half(h)]).then_inc(c_aux.sem, 1)

            def max_tile(i, t, p, k):
                j, n, h = MAX_ORDER[k]
                ps = bank_free(pe, i, (t, "max", p, k))
                if k in (0, 16):
                    aux_read(pe, i, (t, "qk", p, {0: 0, 16: 3}[k]))
                if k in (0, 8):
                    pe.wait_ge(c_hi.sem, c_hi.at(i, 4 * (4 * nth_pair(t, p) + {0: 2, 8: 3}[k])))
                nc.tensor.matmul(ps[:, :], qs[:, p % 2, j, n * P:(n + 1) * P], kk[:, p % 2, j, token_half(h)],
                                 start=True, stop=True).then_inc(c_aux.sem, 1)

            def neg_rows(i, t, p):
                pe.wait_ge(c_mx.sem, c_mx.at(i, 2 * (nth_pair(t, p) + 1)))
                for h in range(2):
                    ps = bank_free(pe, i, (t, "neg", p, h))
                    for n in range(4):
                        last = nc.tensor.matmul(ps[0:HD + 1, n * P:(n + 1) * P], mxw[:, 4 * h + n, 0:HD + 1],
                                                ident[:, :], start=True, stop=True)
                    last.then_inc(c_aux.sem, 1)

            for g in sorted(GATE_TILES):
                gate_tile(None, -1, g)
            for k in range(4):
                qk_tile(None, -1, PAIRS, k)
            for k in range(32):
                max_tile(None, -1, PAIRS, k)
            neg_rows(None, -1, PAIRS)
            with pe.Fori(0, B) as i:
                for t in range(2):

                    def scores(g, j):
                        p, h, m = g // 16, (g // 8) % 2, g % 8
                        n = TILES * t + g
                        if g % 16 == 0 and j == 0:
                            if g:
                                aux_read(pe, i, (t, "neg", p, 1))
                            elif t:
                                aux_read(pe, i, (0, "neg", PAIRS, 1))
                            else:
                                pe.wait_ge(c_free["A"].sem, c_free["A"].at(i, 0))
                        u = 2 * n + j
                        pe.wait_ge(c_exp.sem, c_exp.at(i, max(u - SCORE_BANKS + 1, 0)))
                        o = score_ps[u % SCORE_BANKS][:, :]
                        nc.tensor.matmul(o, kk[:, p % 2, j, m * P:(m + 1) * P], qs[:, p % 2, j, token_half(h)],
                                         start=True, stop=False)
                        last = nc.tensor.matmul(o, kl[:, p % 2, j, m * P:(m + 1) * P], qm[:, p % 2, j, token_half(h)],
                                                start=False, stop=True)
                        last.then_inc(c_score.sem, 1)

                    def prob_v(g):
                        p, ph, m = g // 16, g // 8, g % 8
                        n = TILES * t + g
                        pe.wait_ge(c_exp.sem, c_exp.at(i, 2 * n + 2))
                        if g < NT:
                            aux_read(pe, i, (t, "v", g))
                        if m == 0:
                            pe.wait_ge(c_olo.sem, c_olo.at(i, max(8 * t + ph - 1, 0)))
                        for j in range(2):
                            head = slice((2 * p + j) * HD, (2 * p + j + 1) * HD)
                            last = nc.tensor.matmul(acc_ps[ph % 2][j * HD:(j + 1) * HD, :], v_y[:, m, head],
                                                    probs[:, n % SLOTS_P, token_half(j)],
                                                    start=(m == 0), stop=(m == NT - 1))
                        last.then_inc(c_pv.sem, 1)

                    def denominator(ph):
                        h = ph % 2
                        ps = bank_free(pe, i, (t, "den", ph))
                        pe.wait_ge(c_sum[h].sem, c_sum[h].at(i, NSUM // 2 * t + (NT - 1) * (ph // 2 + 1)))
                        for j in range(2):
                            last = nc.tensor.matmul(ps[j * HD:(j + 1) * HD, :], ones[:, :], sums[h][:, token_half(j)],
                                                    start=True, stop=True)
                        last.then_inc(c_aux.sem, 1)

                    def v_tile(m):
                        ps = bank_free(pe, i, (t, "v", m))
                        halves(ps[:, :], lambda a, k: xs[:, a, k, m * P:(m + 1) * P],
                               lambda b, k: w_vo[:, k // 2, b, k % 2, :]).then_inc(c_aux.sem, 1)

                    def o_tile(k):
                        ps = bank_free(pe, i, (t, "o", k))
                        pe.wait_ge(c_olo.sem, c_olo.at(i, 8 * t + 7 + k // 4))
                        ct = k % 4
                        halves(ps[:, :], lambda a, c: w_vo[:, c // 2, a, c % 2, ct * P:(ct + 1) * P],
                               lambda b, c: o_t[:, b, c, token_half(k // 4)]).then_inc(c_aux.sem, 1)

                    scores(0, 0)
                    scores(0, 1)
                    for k in range(4):
                        qk_tile(i, t, 1, k)
                    pe.wait_ge(c_wv.sem, c_wv.at(i, 16 * 8 * (t + 1)))
                    v_tile(0)
                    for g in range(TILES):
                        todo = maxes(g)
                        if g + 1 < TILES:
                            scores(g + 1, 0)
                        for f in todo[:1]:
                            max_tile(i, t, f[1], f[2])
                        if g + 1 < TILES:
                            scores(g + 1, 1)
                        if g % 16 == NEG:
                            neg_rows(i, t, g // 16 + 1)
                        for f in projection(g):
                            if f[0] == "qk":
                                qk_tile(i, t, f[1], f[2])
                            else:
                                v_tile(f[1])
                        for f in todo[1:2]:
                            max_tile(i, t, f[1], f[2])
                        prob_v(g)
                        for f in todo[2:]:
                            max_tile(i, t, f[1], f[2])
                        if g in DENS:
                            denominator(DENS[g])
                        if t == 1 and g in GATE_TILES:
                            gate_tile(i, t, g)
                    pe.wait_ge(c_wo.sem, c_wo.at(i, 32 * (t + 1)))
                    o_tile(0)
                    denominator(2 * PAIRS - 1)
                    for k in range(1, 8):
                        o_tile(k)


_INS = ["x", "L0_conv_w1", "L0_conv_b1", "L0_conv_w2", "L0_conv_b2",
        "L0_conv_hdn_w_qkv", "L0_conv_hdn_b_qkv", "L0_conv_hdn_w_o", "L0_conv_hdn_b_o",
        "L0_conv_eu_w_qkv", "L0_conv_eu_b_qkv", "L0_conv_eu_w_o", "L0_conv_eu_b_o"]
_OUTS = [((B, C, H, W), "float32")]


def kernel(**inputs):
    import numpy as _np
    import concourse.bacc as _bacc
    from concourse import mybir as _mybir
    from concourse.bass_utils import run_bass_kernel_spmd as _run

    nc = _bacc.Bacc("TRN2", target_bir_lowering=False, num_devices=1)
    arrays, args = {}, []
    for name in _INS:
        a = _np.ascontiguousarray(inputs[name])
        arrays[f"in_{name}_dram"] = a
        args.append(nc.dram_tensor(f"in_{name}_dram", a.shape, _mybir.dt.from_np(a.dtype), kind="ExternalInput").ap())
    for i, (shape, dtype) in enumerate(_OUTS):
        dt = _mybir.dt.from_np(_np.dtype(dtype))
        args.append(nc.dram_tensor(f"out_{i}_dram", shape, dt, kind="ExternalOutput").ap())
    build(nc, *args)
    r = _run(nc, [arrays], core_ids=[0])
    return r.results[0]["out_0_dram"]
```
